# Optimizing a Trainium2 kernel written in Bass

```python
import numpy as np
import jax
import jax.numpy as jnp

def _softmax(x, axis=-1):
    return jax.nn.softmax(x, axis=axis)

def _gelu(x):
    return jax.nn.gelu(x, approximate=True)

def _silu(x):
    return jax.nn.silu(x)

def _sigmoid(x):
    return jax.nn.sigmoid(x)

def _layernorm(x, axis=-1, eps=1e-05):
    m = jnp.mean(x, axis=axis, keepdims=True)
    v = jnp.var(x, axis=axis, keepdims=True)
    return (x - m) / jnp.sqrt(v + eps)

def _scatter_add(tgt, idx, src, axis=0):
    return tgt.at[idx].add(src)

def _segment_sum(src, seg, n):
    return jax.ops.segment_sum(src, seg, n)
kernel_name = 'mk_adj_preln_d2_adj_r2_85e8ca'

def setup_inputs(seed: int=0):
    np.random.seed(seed)
    _w = jnp.asarray

    def _rec_inputs():
        import jax
        import jax.numpy as jnp
        _gk = jax.random.key(seed)
        x = -0.0003929 + 0.9999 * jax.random.normal(jax.random.fold_in(_gk, 1), (32, 256, 256), jnp.float32)
        _w = (1.0 + jnp.arange(256, dtype=jnp.float32)) ** (-0.5)
        _w = _w / _w.mean()
        _pij = jnp.clip(0.03125 * _w[:, None] * _w[None, :], 0.0, 1.0)
        _a = jax.random.uniform(jax.random.fold_in(_gk, 2), (32, 256, 256)) < _pij
        _a = jnp.logical_or(_a, jnp.eye(256, dtype=bool))
        _af = _a.astype(jnp.float32)
        _af = _af * jax.random.uniform(jax.random.fold_in(_gk, 3), (32, 256, 256), jnp.float32, 0.05, 1)
        adj = _af
        return (x, adj)
    x, adj = _rec_inputs()

    def _L0_gnn_setup():
        import jax, jax.numpy as jnp
        import numpy as np
        EPS = 1e-06
        key = jax.random.key(seed)
        k1, k2, k3 = jax.random.split(key, 3)
        B, N, F, O = (8, 2048, 256, 256)
        x = jax.random.normal(k1, (B, N, F), dtype=jnp.float32)
        adj = jax.random.uniform(k2, (B, N, N), dtype=jnp.float32)
        W = jax.random.normal(k3, (O, 2 * F), dtype=jnp.float32) * (1.0 / np.sqrt(2 * F))
        return {'x': x, 'adj': adj, 'W': W}
    _L0_gnn_all = _L0_gnn_setup()
    _L0_gnn_in = {k: v for k, v in _L0_gnn_all.items() if k in ('W',)}
    del _L0_gnn_all

    def _L1_gnn_setup():
        import jax, jax.numpy as jnp
        import numpy as np
        EPS_LN = 1e-05

        def hypergraph_conv(x, adj, W, b):
            N, C, _ = adj.shape
            H = (adj != 0).astype(x.dtype)
            w = adj.reshape(N, -1)[:, :C]
            xw = jnp.einsum('ncd,hd->nch', x, W)
            Dn = jnp.einsum('nce,ne->nc', H, w)
            Dn = jnp.where(Dn > 0, 1.0 / Dn, 0.0)
            Be = H.sum(axis=1)
            Be = jnp.where(Be > 0, 1.0 / Be, 0.0)
            m = Be[:, :, None] * jnp.einsum('nce,nch->neh', H, xw)
            out = Dn[:, :, None] * jnp.einsum('nce,neh->nch', H, m)
            return out + b

        def layer_norm(x, g, b):
            mu = jnp.mean(x, axis=-1, keepdims=True)
            var = jnp.var(x, axis=-1, keepdims=True)
            return (x - mu) * jax.lax.rsqrt(var + EPS_LN) * g + b
        key = jax.random.key(seed)
        ks = jax.random.split(key, 4)
        N, C, Din, Dh, Dout = (16, 512, 256, 512, 256)
        x = jax.random.normal(ks[0], (N, C, Din), dtype=jnp.float32)
        adj = jax.random.uniform(ks[1], (N, C, C), dtype=jnp.float32, minval=0.1, maxval=1.0)
        W1 = jax.random.normal(ks[2], (Dh, Din), dtype=jnp.float32) * (1.0 / np.sqrt(Din))
        b1 = jnp.zeros((Dh,), dtype=jnp.float32)
        gamma = jnp.ones((Dh,), dtype=jnp.float32)
        beta = jnp.zeros((Dh,), dtype=jnp.float32)
        W2 = jax.random.normal(ks[3], (Dout, Dh), dtype=jnp.float32) * (1.0 / np.sqrt(Dh))
        b2 = jnp.zeros((Dout,), dtype=jnp.float32)
        return {'x': x, 'adj': adj, 'W1': W1, 'b1': b1, 'gamma': gamma, 'beta': beta, 'W2': W2, 'b2': b2}
    _L1_gnn_all = _L1_gnn_setup()
    _L1_gnn_in = {k: v for k, v in _L1_gnn_all.items() if k in ('W1', 'b1', 'gamma', 'beta', 'W2', 'b2')}
    del _L1_gnn_all
    return {'x': x, 'adj': adj, 'L0_gnn_W': _L0_gnn_in['W'], 'L1_gnn_W1': _L1_gnn_in['W1'], 'L1_gnn_b1': _L1_gnn_in['b1'], 'L1_gnn_gamma': _L1_gnn_in['gamma'], 'L1_gnn_beta': _L1_gnn_in['beta'], 'L1_gnn_W2': _L1_gnn_in['W2'], 'L1_gnn_b2': _L1_gnn_in['b2']}

def reference(x, adj, L0_gnn_W, L1_gnn_W1, L1_gnn_b1, L1_gnn_gamma, L1_gnn_beta, L1_gnn_W2, L1_gnn_b2):
    import jax
    import jax.numpy as jnp

    def _L0_gnn_ref(x, adj, W):
        import jax, jax.numpy as jnp
        import numpy as np
        EPS = 1e-06
        deg = jnp.sum(adj, axis=-1, keepdims=True)
        agg = jnp.einsum('bij,bjf->bif', adj, x) / jnp.maximum(deg, EPS)
        cat = jnp.concatenate([x, agg], axis=2)
        out = jnp.einsum('bnf,of->bno', cat, W)
        return jax.nn.relu(out)

    def _L1_gnn_ref(x, adj, W1, b1, gamma, beta, W2, b2):
        import jax, jax.numpy as jnp
        import numpy as np
        EPS_LN = 1e-05

        def hypergraph_conv(x, adj, W, b):
            N, C, _ = adj.shape
            H = (adj != 0).astype(x.dtype)
            w = adj.reshape(N, -1)[:, :C]
            xw = jnp.einsum('ncd,hd->nch', x, W)
            Dn = jnp.einsum('nce,ne->nc', H, w)
            Dn = jnp.where(Dn > 0, 1.0 / Dn, 0.0)
            Be = H.sum(axis=1)
            Be = jnp.where(Be > 0, 1.0 / Be, 0.0)
            m = Be[:, :, None] * jnp.einsum('nce,nch->neh', H, xw)
            out = Dn[:, :, None] * jnp.einsum('nce,neh->nch', H, m)
            return out + b

        def layer_norm(x, g, b):
            mu = jnp.mean(x, axis=-1, keepdims=True)
            var = jnp.var(x, axis=-1, keepdims=True)
            return (x - mu) * jax.lax.rsqrt(var + EPS_LN) * g + b
        h = jax.nn.relu(hypergraph_conv(x, adj, W1, b1))
        h = layer_norm(h, gamma, beta)
        y = hypergraph_conv(h, adj, W2, b2)
        return y + x
    h = jnp.maximum(_layernorm(x, axis=-1), 0.0)
    x = x + _L0_gnn_ref(h, adj, L0_gnn_W)
    h = jnp.maximum(_layernorm(x, axis=-1), 0.0)
    x = x + _L1_gnn_ref(h, adj, L1_gnn_W1, L1_gnn_b1, L1_gnn_gamma, L1_gnn_beta, L1_gnn_W2, L1_gnn_b2)
    return x

_drawn_inputs = setup_inputs


def setup_inputs(seed=0):
    import zlib

    import numpy as np

    out = dict(_drawn_inputs(seed))
    spreads = {'L1_gnn_b1': (0.0, 0.1),
     'L1_gnn_gamma': (1.0, 0.2),
     'L1_gnn_beta': (0.0, 0.1),
     'L1_gnn_b2': (0.0, 0.8)}
    factors = {}
    for name, (base, spread) in spreads.items():
        noise = np.random.default_rng([zlib.crc32(name.encode()), seed]).standard_normal(out[name].shape)
        drawn = base * np.exp(spread * noise) if base else spread * noise
        out[name] = jnp.asarray(drawn.astype(out[name].dtype))
    for name, factor in factors.items():
        out[name] = (out[name] * factor).astype(out[name].dtype)
    return out
```

```python
from contextlib import ExitStack

import concourse.bass as bass
from concourse import mybir

ALU = mybir.AluOpType
ACT = mybir.ActivationFunctionType
F32 = mybir.dt.float32
F32R = mybir.dt.float32r

P = 128
EPS_LN = 1e-5
EPS_DEG = 1e-6
TINY = 1.1754944e-38


class Graph:

    def __init__(self, round_, off, total):
        self.round, self.off, self.total = round_, off, total
        self.slot = off % 2
        self.exists = not isinstance(round_, int) or 0 <= off < total

    def plus(self, n):
        return Graph(self.round, self.off + n, self.total)

    def index(self):
        return self.round * 2 + self.off

    def count(self, per, part=None):
        return self.round * (2 * per) + (per * self.off + (per if part is None else part))

    def dma_count(self):
        return self.round * 16 + 16 * (self.off // 2 + 1)


def gnn_two_layers_kernel(nc, x, adjT, WabT, W1T, b1, gamma, beta, W2T, b2, out):
    B, N, F = x.shape
    O2 = WabT.shape[1]
    HID = W1T.shape[1]
    NC, HC = N // P, HID // P
    assert N == F == 2 * P and O2 == 2 * F and HID == 4 * P and B % 2 == 0

    x_v = x.rearrange("b (c p) f -> b p c f", p=P)
    adjT_v = adjT.rearrange("b (c p) n -> b p c n", p=P)
    out_v = out.rearrange("b (c p) f -> b p c f", p=P)

    with ExitStack() as ctx:
        def sb(name, shape, dt=F32):
            return ctx.enter_context(nc.sbuf_tensor(name, shape, dt))

        def sem(name):
            return ctx.enter_context(nc.semaphore(name))

        ident = sb("ident", [P, P])
        ones = sb("ones", [P, P])
        per_hidden = sb("per_hidden", [P, P])
        neg_half, neg_one, eps_ln = (sb(n, [P, NC]) for n in ("neg_half", "neg_one", "eps_ln"))
        WabT_raw = sb("WabT_raw", [P, NC, O2])
        W1T_raw = sb("W1T_raw", [P, NC, HID])
        W2T_raw = sb("W2T_raw", [P, HC, F])
        gamma_s = sb("gamma_s", [P, HC])
        beta_s = sb("beta_s", [P, HC])
        beta_bc = sb("beta_bc", [P, HC, P])
        W2g = sb("W2g", [P, HC, F])
        W2c = sb("W2c", [P, HC, F])
        Wab_hi, Wab_lo = sb("Wab_hi", [P, NC, O2], F32R), sb("Wab_lo", [P, NC, O2], F32R)
        W1_hi, W1_lo = sb("W1_hi", [P, NC, HID], F32R), sb("W1_lo", [P, NC, HID], F32R)
        W2_hi, W2_lo = sb("W2_hi", [P, HC, F], F32R), sb("W2_lo", [P, HC, F], F32R)
        b1_bc = sb("b1_bc", [P, HID])
        b2_bc = sb("b2_bc", [P, NC, F])
        cb_bc = sb("cb_bc", [P, F])

        x_s = [sb(f"x_s{i}", [P, NC, F]) for i in range(2)]
        adjT_s = [sb(f"adjT_s{i}", [P, NC, N]) for i in range(2)]
        adj_hi, adj_lo = sb("adj_hi", [P, NC, N], F32R), sb("adj_lo", [P, NC, N], F32R)
        stats1, mv1 = sb("stats1", [P, NC, 6]), sb("mv1", [P, NC, 2])
        ve1, nm1, rstd1 = sb("ve1", [P, NC]), sb("nm1", [P, NC]), sb("rstd1", [P, NC])
        z1 = sb("z1", [P, NC, F])
        hT_hi, hT_lo = sb("hT_hi", [P, NC, N], F32R), sb("hT_lo", [P, NC, N], F32R)
        V_hi, V_lo = sb("V_hi", [P, NC, F + 2], F32R), sb("V_lo", [P, NC, F], F32R)
        Q1 = sb("Q1", [P, NC, F])
        deg, rdeg = sb("deg", [P, NC]), sb("rdeg", [P, NC])
        agg = sb("agg", [P, NC, F])
        x1 = sb("x1", [P, NC, F])
        stats2, mv2 = sb("stats2", [P, NC, 6]), sb("mv2", [P, NC, 2])
        ve2, nm2, rstd2, nmr2 = (sb(n, [P, NC]) for n in ("ve2", "nm2", "rstd2", "nmr2"))
        h2 = sb("h2", [P, NC, F])
        h2_hi, h2_lo = sb("h2_hi", [P, NC, F], F32R), sb("h2_lo", [P, NC, F], F32R)
        HT = sb("HT", [P, NC, N], F32R)
        cnt, cnt1, Be = sb("cnt", [P, NC]), sb("cnt1", [P, NC]), sb("Be", [P, NC])
        B_hi, B_lo = sb("B_hi", [P, NC, N + 2], F32R), sb("B_lo", [P, NC, N + 2], F32R)
        A_hi = [sb(f"A_hi{i}", [P, NC, N], F32R) for i in range(2)]
        A_lo = [sb(f"A_lo{i}", [P, NC, N], F32R) for i in range(2)]
        D, Drec = sb("D", [P, NC]), sb("Drec", [P, NC])
        Dn = [sb(f"Dn{i}", [P, NC]) for i in range(2)]
        uT_hi, uT_lo = sb("uT_hi", [P, NC, N], F32R), sb("uT_lo", [P, NC, N], F32R)
        g = sb("g", [P, NC, HID])
        stats3, mv3 = sb("stats3", [P, NC, 6]), sb("mv3", [P, NC, 2])
        ve3, rstd3 = sb("ve3", [P, NC]), sb("rstd3", [P, NC])
        gT_hi, gT_lo = sb("gT_hi", [P, NC, HC, P], F32R), sb("gT_lo", [P, NC, HC, P], F32R)
        q = sb("q", [P, NC, F])
        q_hi, q_lo = sb("q_hi", [P, NC, F], F32R), sb("q_lo", [P, NC, F], F32R)
        y = [sb(f"y{i}", [P, NC, F]) for i in range(2)]

        bank = [ctx.enter_context(nc.psum_tensor(f"bank{i}", [P, 512], F32)) for i in range(8)]

        def chunks(t):
            return t[:, :].rearrange("p (c n) -> p c n", c=NC)

        ps_uT, ps_y, ps_T, ps_q = chunks(bank[0]), chunks(bank[1]), chunks(bank[7]), chunks(bank[4])
        ps_gT = [bank[c][:, :].rearrange("p (o n) -> p o n", o=HC) for c in (0, 1)]
        ps_w1 = [bank[2], bank[3]]
        ps_A = [bank[2], bank[3]]
        ps_R = [bank[4], bank[5]]
        ps_QV = [bank[5], bank[6]]
        ps_mean, ps_cb = bank[2], bank[3]

        wab_loaded, w1_loaded, w2_loaded, rows_loaded = map(sem, ("wab_loaded", "w1_loaded", "w2_loaded", "rows_loaded"))
        x_loaded = [sem(f"x_loaded{i}") for i in range(2)]
        adj_loaded = [sem(f"adj_loaded{i}") for i in range(2)]
        y_stored = [sem(f"y_stored{i}") for i in range(2)]
        names = ("const_zeroed const_ready "
                 "wab_hi_ready wab_ready w1_hi_ready w1_ready w2_scaled w2_sums_ready w2_centred w2_hi_ready w2_ready "
                 "T_ready QV_ready R_ready A_ready uT_ready w1out_ready gT_ready q_ready y_ready "
                 "adj_hi_ready QV_copied uT_hi_ready B_hi_ready g_ready hT_hi_ready gT_hi_ready A_hi_ready "
                 "h2_ready q_hi_ready "
                 "V_lo_ready stats1_ready mv1_ready uT_lo_ready HT_ready cnt1_ready Be_ready y_done conv1_ready "
                 "B_lo_ready stats3_ready mv3_ready deg_ready rdeg_ready agg_ready gT_lo_ready x1_ready "
                 "stats2_ready mv2_ready hT_lo_ready A_lo_ready Drec_ready Dn_ready h2_hi_ready qf_ready "
                 "adj_lo_ready w_lo_ready ve1_ready rstd1_ready z1_ready ve3_ready rstd3_ready ve2_ready rstd2_ready "
                 "norm2_ready x1b_ready h2_lo_ready q_lo_ready ypart_ready").split()
        s = {n: sem(n) for n in names}
        (const_zeroed, const_ready,
         wab_hi_ready, wab_ready, w1_hi_ready, w1_ready, w2_scaled, w2_sums_ready, w2_centred, w2_hi_ready, w2_ready,
         T_ready, QV_ready, R_ready, A_ready, uT_ready, w1out_ready, gT_ready, q_ready, y_ready,
         adj_hi_ready, QV_copied, uT_hi_ready, B_hi_ready, g_ready, hT_hi_ready, gT_hi_ready, A_hi_ready,
         h2_ready, q_hi_ready,
         V_lo_ready, stats1_ready, mv1_ready, uT_lo_ready, HT_ready, cnt1_ready, Be_ready, y_done, conv1_ready,
         B_lo_ready, stats3_ready, mv3_ready, deg_ready, rdeg_ready, agg_ready, gT_lo_ready, x1_ready,
         stats2_ready, mv2_ready, hT_lo_ready, A_lo_ready, Drec_ready, Dn_ready, h2_hi_ready, qf_ready,
         adj_lo_ready, w_lo_ready, ve1_ready, rstd1_ready, z1_ready, ve3_ready, rstd3_ready, ve2_ready, rstd2_ready,
         norm2_ready, x1b_ready, h2_lo_ready, q_lo_ready, ypart_ready) = (s[n] for n in names)

        LOOP_FROM, LOOP_ROUNDS = 1, (B - 4) // 2

        def run(eng, step, before=None):
            for b in range(-2, LOOP_FROM):
                if before and b in before:
                    before[b]()
                step(Graph(0, b, B))
            with eng.Fori(0, LOOP_ROUNDS) as r:
                for j in range(2):
                    step(Graph(r, LOOP_FROM + j, B))
            for b in range(LOOP_FROM + 2 * LOOP_ROUNDS, B + 1):
                step(Graph(0, b, B))

        block = ctx.enter_context(nc.Block())

        @block.sync
        def _(sp):
            def load_adj(k):
                sp.dma_start(adjT_s[k.slot][:, :, :], adjT_v[k.index()]).then_inc(adj_loaded[k.slot], 16)

            def load_x(k):
                sp.dma_start(x_s[k.slot][:, :, :], x_v[k.index()]).then_inc(x_loaded[k.slot], 16)

            def weights():
                load_x(Graph(0, 0, B))
                load_adj(Graph(0, 0, B))
                sp.dma_start(WabT_raw[:, :, :], WabT.rearrange("(c p) o -> p c o", p=P)).then_inc(wab_loaded, 16)

            def more_weights():
                sp.dma_start(W1T_raw[:, :, :], W1T.rearrange("(c p) o -> p c o", p=P)).then_inc(w1_loaded, 16)
                sp.dma_start(W2T_raw[:, :, :], W2T.rearrange("(c p) o -> p c o", p=P)).then_inc(w2_loaded, 16)
                sp.dma_start(gamma_s[:, :], gamma).then_inc(rows_loaded, 16)
                sp.dma_start(beta_s[:, :], beta).then_inc(rows_loaded, 16)
                sp.dma_start(b1_bc[:, :], b1.partition_broadcast(P)).then_inc(rows_loaded, 16)
                for c in range(NC):
                    sp.dma_start(b2_bc[:, c, :], b2.partition_broadcast(P)).then_inc(rows_loaded, 16)

            def step(b):
                done, first, ahead = b.plus(-1), b.plus(1), b.plus(3)
                if done.exists:
                    sp.wait_ge(y_done, done.count(1))
                    sp.dma_start(out_v[done.index()], y[done.slot][:, :, :]).then_inc(y_stored[done.slot], 16)
                if ahead.exists:
                    if first.exists:
                        sp.wait_ge(B_hi_ready, first.count(1))
                        sp.wait_ge(w_lo_ready, first.count(1))
                    load_adj(ahead)
                    if first.exists:
                        sp.wait_ge(x1_ready, first.count(1))
                    load_x(ahead)

            run(sp, step, {-2: weights, -1: more_weights})
            for k in (B - 2, B - 1):
                sp.wait_ge(y_stored[k % 2], Graph(0, k, B).dma_count())

        @block.gpsimd
        def _(pool):
            def constants():
                pool.memset(ident[:, :], 0.0).then_inc(const_zeroed, 1)
                pool.memset(ones[:, :], 1.0)
                pool.memset(per_hidden[:, :], 1.0 / HID)
                pool.memset(neg_half[:, :], -0.5)
                pool.memset(neg_one[:, :], -1.0)
                pool.memset(eps_ln[:, :], EPS_LN)
                pool.memset(V_hi[:, :, F:F + 2].bitcast(F32), 1.0)
                pool.memset(B_hi[:, :, N:N + 2].bitcast(F32), 0.0)
                pool.memset(B_lo[:, :, N:N + 2].bitcast(F32), 0.0).then_inc(const_zeroed, 1)
                pool.wait_ge(const_zeroed, 2)
                pool.affine_select(out=ident[:, :], in_=ident[:, :], compare_op=ALU.not_equal, fill=1.0,
                                   base=0, pattern=[[-1, P]], channel_multiplier=1).then_inc(const_ready, 1)
                pool.wait_ge(const_ready, 1)

            def step(b):
                done, first, ahead = b.plus(-1), b.plus(1), b.plus(2)
                if ahead.exists:
                    pool.wait_ge(mv1_ready, ahead.count(1))
                    pool.tensor_tensor(ve1[:, :], mv1[:, :, 1], eps_ln[:, :], ALU.add)
                    pool.tensor_tensor(nm1[:, :], mv1[:, :, 0], neg_one[:, :], ALU.mult).then_inc(ve1_ready, 1)
                    pool.wait_ge(ve1_ready, ahead.count(1))
                    pool.tensor_tensor(rstd1[:, :], ve1[:, :], neg_half[:, :], ALU.pow).then_inc(rstd1_ready, 1)
                    pool.wait_ge(rstd1_ready, ahead.count(1))
                    if first.exists:
                        pool.wait_ge(T_ready, first.count(1))
                if first.exists:
                    pool.wait_ge(adj_hi_ready, first.count(1))
                    pool.tensor_tensor(adj_lo[:, :, :], adjT_s[first.slot][:, :, :], adj_hi[:, :, :].bitcast(F32),
                                       ALU.subtract).then_inc(adj_lo_ready, 1)
                    pool.tensor_tensor(B_lo[:, :, N:N + 1], adjT_s[first.slot][:, :, 0:1],
                                       adj_hi[:, :, 0:1].bitcast(F32), ALU.subtract).then_inc(w_lo_ready, 1)
                if ahead.exists:
                    for c in range(NC):
                        z = pool.tensor_scalar(z1[:, c, :], x_s[ahead.slot][:, c, :], nm1[:, c:c + 1],
                                               rstd1[:, c:c + 1], ALU.add, ALU.mult)
                    z.then_inc(z1_ready, 1)
                if b.exists:
                    pool.wait_ge(mv3_ready, b.count(1))
                    pool.tensor_tensor(ve3[:, :], mv3[:, :, 1], eps_ln[:, :], ALU.add).then_inc(ve3_ready, 1)
                    pool.wait_ge(ve3_ready, b.count(1))
                    pool.tensor_tensor(rstd3[:, :], ve3[:, :], neg_half[:, :], ALU.pow).then_inc(rstd3_ready, 1)
                if first.exists:
                    pool.wait_ge(mv2_ready, first.count(1))
                    pool.tensor_tensor(ve2[:, :], mv2[:, :, 1], eps_ln[:, :], ALU.add)
                    pool.tensor_tensor(nm2[:, :], mv2[:, :, 0], neg_one[:, :], ALU.mult).then_inc(ve2_ready, 1)
                    pool.wait_ge(ve2_ready, first.count(1))
                    pool.tensor_tensor(rstd2[:, :], ve2[:, :], neg_half[:, :], ALU.pow).then_inc(rstd2_ready, 1)
                    pool.wait_ge(rstd2_ready, first.count(1))
                    pool.tensor_tensor(nmr2[:, :], nm2[:, :], rstd2[:, :], ALU.mult).then_inc(norm2_ready, 1)
                    if done.exists:
                        pool.wait_ge(y_stored[done.slot], done.dma_count())
                    if first.off == 0 and isinstance(first.round, int):
                        pool.wait_ge(rows_loaded, 16 * (3 + NC))
                    pool.tensor_tensor(y[first.slot][:, :, :], x1[:, :, :], b2_bc[:, :, :],
                                       ALU.add).then_inc(x1b_ready, 1)
                    pool.wait_ge(h2_hi_ready, first.count(1))
                    if b.exists:
                        pool.wait_ge(uT_ready, b.count(1))
                    pool.tensor_tensor(h2_lo[:, :, :], h2[:, :, :], h2_hi[:, :, :].bitcast(F32),
                                       ALU.subtract).then_inc(h2_lo_ready, 1)
                if b.exists:
                    pool.wait_ge(q_hi_ready, b.count(1))
                    pool.tensor_tensor(q_lo[:, :, :], q[:, :, :], q_hi[:, :, :].bitcast(F32),
                                       ALU.subtract).then_inc(q_lo_ready, 1)
                if first.exists:
                    pool.wait_ge(x1b_ready, first.count(1))
                    pool.tensor_tensor(y[first.slot][:, :, :], y[first.slot][:, :, :], h2[:, :, :],
                                       ALU.add).then_inc(ypart_ready, 1)

            run(pool, step, {-2: constants})

        @block.scalar
        def _(act):
            def wab():
                act.wait_ge(wab_loaded, 16)
                act.activation(Wab_hi[:, :, :], WabT_raw[:, :, :], ACT.Copy).then_inc(wab_hi_ready, 1)

            def w1():
                act.wait_ge(w1_loaded, 16)
                act.activation(W1_hi[:, :, :], W1T_raw[:, :, :], ACT.Copy).then_inc(w1_hi_ready, 1)

            def step(b):
                done, first, ahead = b.plus(-1), b.plus(1), b.plus(2)
                if first.exists:
                    act.wait_ge(adj_loaded[first.slot], first.dma_count())
                    if b.exists:
                        act.wait_ge(A_ready, b.count(NC))
                    act.activation(adj_hi[:, :, :], adjT_s[first.slot][:, :, :], ACT.Copy).then_inc(adj_hi_ready, 1)
                    for c in range(NC):
                        act.wait_ge(QV_ready, first.count(NC, c + 1))
                        if b.exists and c == 0:
                            act.wait_ge(agg_ready, b.count(1))
                        act.activation(V_hi[:, c, 0:F], ps_QV[c][:, F:2 * F], ACT.Copy)
                        act.activation(Q1[:, c, :], ps_QV[c][:, 0:F], ACT.Copy).then_inc(QV_copied, 1)
                if b.exists:
                    act.wait_ge(uT_ready, b.count(1))
                    if done.exists:
                        act.wait_ge(w1out_ready, done.count(NC))
                    act.activation(uT_hi[:, :, :], ps_uT, ACT.Copy).then_inc(uT_hi_ready, 1)
                if first.exists:
                    act.wait_ge(Be_ready, first.count(1))
                    act.activation(B_hi[:, :, N:N + 1], adjT_s[first.slot][:, :, 0:1], ACT.Copy)
                    for c in range(NC):
                        i = act.activation(B_hi[:, c, 0:N], HT[:, c, :].bitcast(F32), ACT.Copy, scale=Be[:, c:c + 1])
                    i.then_inc(B_hi_ready, 1)
                if b.exists:
                    for c in range(NC):
                        act.wait_ge(conv1_ready, b.count(NC, c + 1))
                        act.activation(g[:, c, :], g[:, c, :], ACT.Relu).then_inc(g_ready, 1)
                if ahead.exists:
                    act.wait_ge(T_ready, ahead.count(1))
                    if first.exists:
                        act.wait_ge(QV_ready, first.count(NC))
                    act.activation(hT_hi[:, :, :], ps_T, ACT.Relu).then_inc(hT_hi_ready, 1)
                if b.exists:
                    for c in range(NC):
                        act.wait_ge(gT_ready, b.count(NC, c + 1))
                        if done.exists:
                            act.wait_ge(q_ready, done.count(1))
                        act.activation(gT_hi[:, c, :, :], ps_gT[c], ACT.Copy).then_inc(gT_hi_ready, 1)
                if first.exists:
                    for c in range(NC):
                        act.wait_ge(A_ready, first.count(NC, c + 1))
                        if done.exists and c == 0:
                            act.wait_ge(y_ready, done.count(1))
                        act.activation(A_hi[first.slot][:, c, :], ps_A[c][:, 0:N], ACT.Copy).then_inc(A_hi_ready, 1)
                    act.wait_ge(norm2_ready, first.count(1))
                    if b.exists:
                        act.wait_ge(ypart_ready, b.count(1))
                    for c in range(NC):
                        i = act.activation(h2[:, c, :], x1[:, c, :], ACT.Relu, scale=rstd2[:, c:c + 1],
                                           bias=nmr2[:, c:c + 1])
                    i.then_inc(h2_ready, 1)
                if b.exists:
                    act.wait_ge(qf_ready, b.count(1))
                    act.activation(q_hi[:, :, :], q[:, :, :], ACT.Copy).then_inc(q_hi_ready, 1)

            run(act, step, {-2: wab, -1: w1})

        @block.vector
        def _(dve):
            def wab():
                dve.wait_ge(wab_hi_ready, 1)
                dve.tensor_tensor(Wab_lo[:, :, :], WabT_raw[:, :, :], Wab_hi[:, :, :].bitcast(F32),
                                  ALU.subtract).then_inc(wab_ready, 1)

            def w1_w2():
                dve.wait_ge(w1_hi_ready, 1)
                dve.tensor_tensor(W1_lo[:, :, :], W1T_raw[:, :, :], W1_hi[:, :, :].bitcast(F32),
                                  ALU.subtract).then_inc(w1_ready, 1)
                dve.wait_ge(w2_loaded, 16)
                dve.wait_ge(rows_loaded, 16 * (3 + NC))
                dve.wait_ge(const_ready, 1)
                for o in range(HC):
                    dve.tensor_scalar(W2g[:, o, :], W2T_raw[:, o, :], gamma_s[:, o:o + 1], None, ALU.mult)
                    i = dve.tensor_scalar(beta_bc[:, o, :], ones[:, :], beta_s[:, o:o + 1], None, ALU.mult)
                i.then_inc(w2_scaled, 1)
                dve.wait_ge(w2_sums_ready, 1)
                for o in range(HC):
                    dve.tensor_tensor(W2c[:, o, :], W2g[:, o, :], ps_mean[:, 0:F], ALU.subtract)
                dve.tensor_copy(cb_bc[:, :], ps_cb[:, 0:F]).then_inc(w2_centred, 1)
                dve.wait_ge(w2_centred, 1)
                dve.tensor_copy(W2_hi[:, :, :], W2c[:, :, :]).then_inc(w2_hi_ready, 1)
                dve.wait_ge(w2_hi_ready, 1)
                dve.tensor_tensor(W2_lo[:, :, :], W2c[:, :, :], W2_hi[:, :, :].bitcast(F32),
                                  ALU.subtract).then_inc(w2_ready, 1)

            def step(b):
                done, first, ahead = b.plus(-1), b.plus(1), b.plus(2)
                if first.exists:
                    for c in range(NC):
                        dve.wait_ge(QV_copied, first.count(NC, c + 1))
                        dve.tensor_tensor(V_lo[:, c, :], ps_QV[c][:, F:2 * F], V_hi[:, c, 0:F].bitcast(F32),
                                          ALU.subtract).then_inc(V_lo_ready, 1)
                if ahead.exists:
                    dve.wait_ge(x_loaded[ahead.slot], ahead.dma_count())
                    for c in range(NC):
                        i = dve.bn_stats(stats1[:, c, :], x_s[ahead.slot][:, c, :])
                    i.then_inc(stats1_ready, 1)
                    dve.wait_ge(stats1_ready, ahead.count(1))
                if b.exists:
                    dve.wait_ge(uT_hi_ready, b.count(1))
                    dve.tensor_tensor(uT_lo[:, :, :], ps_uT, uT_hi[:, :, :].bitcast(F32),
                                      ALU.subtract).then_inc(uT_lo_ready, 1)
                if ahead.exists:
                    for c in range(NC):
                        i = dve.bn_aggr(mv1[:, c, :], stats1[:, c, :])
                    i.then_inc(mv1_ready, 1)
                if first.exists:
                    dve.wait_ge(adj_loaded[first.slot], first.dma_count())
                    if b.exists:
                        dve.wait_ge(A_ready, b.count(NC))
                    for c in range(NC):
                        i = dve.tensor_scalar(HT[:, c, :], adjT_s[first.slot][:, c, :], 0.0, None, ALU.not_equal,
                                              ALU.add, accum_out=cnt[:, c:c + 1])
                    i.then_inc(HT_ready, 1)
                    dve.wait_ge(HT_ready, first.count(1))
                    dve.tensor_scalar(cnt1[:, :], cnt[:, :], 1.0, None, ALU.max).then_inc(cnt1_ready, 1)
                    dve.wait_ge(cnt1_ready, first.count(1))
                    dve.reciprocal(Be[:, :], cnt1[:, :]).then_inc(Be_ready, 1)
                if done.exists:
                    dve.wait_ge(y_ready, done.count(1))
                    dve.wait_ge(ypart_ready, done.count(1))
                    for c in range(NC):
                        i = dve.scalar_tensor_tensor(out=y[done.slot][:, c, :], in0=ps_y[:, c, :],
                                                     scalar=Dn[done.slot][:, c:c + 1], in1=y[done.slot][:, c, :],
                                                     op0=ALU.mult, op1=ALU.add)
                    i.then_inc(y_done, 1)

                def conv1(c):
                    dve.wait_ge(w1out_ready, b.count(NC, c + 1))
                    if done.exists:
                        dve.wait_ge(gT_ready, done.count(NC, c + 1))
                    dve.scalar_tensor_tensor(out=g[:, c, :], in0=ps_w1[c][:, :], scalar=Dn[b.slot][:, c:c + 1],
                                             in1=b1_bc[:, :], op0=ALU.mult, op1=ALU.add).then_inc(conv1_ready, 1)

                if b.exists:
                    dve.wait_ge(Dn_ready, b.count(1))
                    conv1(0)
                if first.exists:
                    dve.wait_ge(B_hi_ready, first.count(1))
                    for c in range(NC):
                        i = dve.scalar_tensor_tensor(out=B_lo[:, c, 0:N], in0=HT[:, c, :].bitcast(F32),
                                                     scalar=Be[:, c:c + 1], in1=B_hi[:, c, 0:N].bitcast(F32),
                                                     op0=ALU.mult, op1=ALU.subtract)
                    i.then_inc(B_lo_ready, 1)
                if b.exists:
                    conv1(1)
                    for c in range(NC):
                        dve.wait_ge(g_ready, b.count(NC, c + 1))
                        i = dve.bn_stats(stats3[:, c, :], g[:, c, :])
                    i.then_inc(stats3_ready, 1)
                    dve.wait_ge(stats3_ready, b.count(1))
                if first.exists:
                    for c in range(NC):
                        dve.wait_ge(R_ready, first.count(NC, c + 1))
                        i = dve.tensor_scalar(deg[:, c:c + 1], ps_R[c][:, F:F + 1], EPS_DEG, None, ALU.max)
                    i.then_inc(deg_ready, 1)
                if b.exists:
                    for c in range(NC):
                        i = dve.bn_aggr(mv3[:, c, :], stats3[:, c, :])
                    i.then_inc(mv3_ready, 1)
                if first.exists:
                    dve.wait_ge(deg_ready, first.count(1))
                    dve.reciprocal(rdeg[:, :], deg[:, :]).then_inc(rdeg_ready, 1)
                    dve.wait_ge(rdeg_ready, first.count(1))
                    for c in range(NC):
                        i = dve.scalar_tensor_tensor(out=agg[:, c, :], in0=ps_R[c][:, 0:F], scalar=rdeg[:, c:c + 1],
                                                     in1=Q1[:, c, :], op0=ALU.mult, op1=ALU.add)
                    i.then_inc(agg_ready, 1)
                if b.exists:
                    for c in range(NC):
                        dve.wait_ge(gT_hi_ready, b.count(NC, c + 1))
                        dve.tensor_tensor(gT_lo[:, c, :, :], ps_gT[c], gT_hi[:, c, :, :].bitcast(F32),
                                          ALU.subtract).then_inc(gT_lo_ready, 1)
                if first.exists:
                    dve.wait_ge(agg_ready, first.count(1))
                    if b.exists:
                        dve.wait_ge(ypart_ready, b.count(1))
                    dve.scalar_tensor_tensor(out=x1[:, :, :], in0=agg[:, :, :], scalar=0.0,
                                             in1=x_s[first.slot][:, :, :], op0=ALU.max,
                                             op1=ALU.add).then_inc(x1_ready, 1)
                    dve.wait_ge(x1_ready, first.count(1))
                    for c in range(NC):
                        i = dve.bn_stats(stats2[:, c, :], x1[:, c, :])
                    i.then_inc(stats2_ready, 1)
                    dve.wait_ge(stats2_ready, first.count(1))
                if ahead.exists:
                    dve.wait_ge(hT_hi_ready, ahead.count(1))
                    dve.scalar_tensor_tensor(out=hT_lo[:, :, :], in0=ps_T, scalar=0.0, in1=hT_hi[:, :, :].bitcast(F32),
                                             op0=ALU.max, op1=ALU.subtract).then_inc(hT_lo_ready, 1)
                if first.exists:
                    for c in range(NC):
                        i = dve.bn_aggr(mv2[:, c, :], stats2[:, c, :])
                    i.then_inc(mv2_ready, 1)
                    for c in range(NC):
                        dve.wait_ge(A_hi_ready, first.count(NC, c + 1))
                        dve.tensor_scalar(D[:, c:c + 1], ps_A[c][:, N:N + 1], TINY, None, ALU.max)
                        dve.tensor_tensor(A_lo[first.slot][:, c, :], ps_A[c][:, 0:N],
                                          A_hi[first.slot][:, c, :].bitcast(F32), ALU.subtract).then_inc(A_lo_ready, 1)
                    dve.wait_ge(A_lo_ready, first.count(NC))
                    dve.reciprocal(Drec[:, :], D[:, :]).then_inc(Drec_ready, 1)
                    dve.wait_ge(Drec_ready, first.count(1))
                    dve.scalar_tensor_tensor(out=Dn[first.slot][:, :], in0=D[:, :], scalar=TINY, in1=Drec[:, :],
                                             op0=ALU.is_gt, op1=ALU.mult).then_inc(Dn_ready, 1)
                    dve.wait_ge(h2_ready, first.count(1))
                    dve.tensor_copy(h2_hi[:, :, :], h2[:, :, :]).then_inc(h2_hi_ready, 1)
                if b.exists:
                    dve.wait_ge(q_ready, b.count(1))
                    dve.wait_ge(rstd3_ready, b.count(1))
                    for c in range(NC):
                        i = dve.scalar_tensor_tensor(out=q[:, c, :], in0=ps_q[:, c, :], scalar=rstd3[:, c:c + 1],
                                                     in1=cb_bc[:, :], op0=ALU.mult, op1=ALU.add)
                    i.then_inc(qf_ready, 1)

            run(dve, step, {-2: wab, 0: w1_w2})

        @block.tensor
        def _(pe):
            def product(out_, pairs, last_sem=None):
                for n, (lhsT, rhs) in enumerate(pairs):
                    width = rhs.shape[-1]
                    i = pe.matmul(out_[:, 0:width], lhsT, rhs, start=n == 0, stop=n == len(pairs) - 1)
                return i

            def w2_sums():
                pe.wait_ge(w2_scaled, 1)
                pe.wait_ge(A_lo_ready, NC)
                product(ps_mean, [(per_hidden[:, :], W2g[:, o, :]) for o in range(HC)])
                product(ps_cb, [(beta_bc[:, o, :], W2T_raw[:, o, :]) for o in range(HC)]).then_inc(w2_sums_ready, 1)

            def start():
                pe.wait_ge(const_ready, 1)

            def step(b):
                done, first, ahead = b.plus(-1), b.plus(1), b.plus(2)

                def part(c):
                    return slice(c * P, (c + 1) * P)

                if b.exists:
                    pe.wait_ge(h2_lo_ready, b.count(1))
                    pe.wait_ge(A_lo_ready, b.count(NC))
                    if done.exists:
                        pe.wait_ge(gT_lo_ready, done.count(NC))
                    hi, lo = A_hi[b.slot], A_lo[b.slot]
                    for f in range(NC):
                        i = product(ps_uT[:, f, :], [
                            pair for c in range(NC) for pair in (
                                (h2_hi[:, c, part(f)], hi[:, c, :]), (h2_hi[:, c, part(f)], lo[:, c, :]),
                                (h2_lo[:, c, part(f)], hi[:, c, :]))])
                    i.then_inc(uT_ready, 1)
                if done.exists:
                    pe.wait_ge(q_lo_ready, done.count(1))
                    if not b.exists:
                        pe.wait_ge(gT_lo_ready, done.count(NC))
                    hi, lo = A_hi[done.slot], A_lo[done.slot]
                    for c in range(NC):
                        i = product(ps_y[:, c, :], [
                            pair for k in range(NC) for pair in (
                                (hi[:, k, part(c)], q_hi[:, k, :]), (hi[:, k, part(c)], q_lo[:, k, :]),
                                (lo[:, k, part(c)], q_hi[:, k, :]))])
                    i.then_inc(y_ready, 1)
                if b.exists:
                    pe.wait_ge(uT_lo_ready, b.count(1))
                    if not done.exists:
                        pe.wait_ge(w2_centred, 1)
                        pe.wait_ge(w1_ready, 1)
                    for c in range(NC):
                        product(ps_w1[c], [
                            pair for f in range(NC) for pair in (
                                (uT_hi[:, f, part(c)], W1_hi[:, f, :]), (uT_hi[:, f, part(c)], W1_lo[:, f, :]),
                                (uT_lo[:, f, part(c)], W1_hi[:, f, :]))]).then_inc(w1out_ready, 1)
                if first.exists:
                    pe.wait_ge(V_lo_ready, first.count(NC))
                    pe.wait_ge(adj_lo_ready, first.count(1))
                    if done.exists:
                        pe.wait_ge(qf_ready, done.count(1))
                    for c in range(NC):
                        product(ps_R[c], [
                            pair for k in range(NC) for pair in (
                                (adj_hi[:, k, part(c)], V_hi[:, k, :]), (adj_hi[:, k, part(c)], V_lo[:, k, :]),
                                (adj_lo[:, k, part(c)], V_hi[:, k, :]))]).then_inc(R_ready, 1)
                if ahead.exists:
                    pe.wait_ge(z1_ready, ahead.count(1))
                    if first.exists:
                        pe.wait_ge(hT_lo_ready, first.count(1))
                    for f in range(NC):
                        for c in range(NC):
                            i = pe.transpose(ps_T[:, f, part(c)], z1[:, c, part(f)], ident[:, :])
                    i.then_inc(T_ready, 1)
                if b.exists:
                    for c in range(NC):
                        pe.wait_ge(g_ready, b.count(NC, c + 1))
                        if done.exists and c == 1:
                            pe.wait_ge(y_done, done.count(1))
                        for o in range(HC):
                            i = pe.transpose(ps_gT[c][:, o, :], g[:, c, part(o)], ident[:, :])
                        i.then_inc(gT_ready, 1)
                if first.exists:
                    pe.wait_ge(B_lo_ready, first.count(1))
                    pe.wait_ge(w_lo_ready, first.count(1))
                    if b.exists:
                        pe.wait_ge(conv1_ready, b.count(NC))
                    for c in range(NC):
                        product(ps_A[c], [
                            pair for e in range(NC) for pair in (
                                (HT[:, e, part(c)], B_hi[:, e, :]), (HT[:, e, part(c)], B_lo[:, e, :]))]
                                ).then_inc(A_ready, 1)
                if b.exists:
                    if first.exists:
                        pe.wait_ge(agg_ready, first.count(1))
                    if not done.exists:
                        pe.wait_ge(w2_ready, 1)
                    for c in range(NC):
                        pe.wait_ge(gT_lo_ready, b.count(NC, c + 1))
                        i = product(ps_q[:, c, :], [
                            pair for o in range(HC) for pair in (
                                (gT_hi[:, c, o, :], W2_hi[:, o, :]), (gT_hi[:, c, o, :], W2_lo[:, o, :]),
                                (gT_lo[:, c, o, :], W2_hi[:, o, :]))])
                    i.then_inc(q_ready, 1)
                if ahead.exists:
                    pe.wait_ge(hT_lo_ready, ahead.count(1))
                    if first.exists:
                        pe.wait_ge(agg_ready, first.count(1))
                    else:
                        pe.wait_ge(wab_ready, 1)
                    for c in range(NC):
                        product(ps_QV[c], [
                            pair for f in range(NC) for pair in (
                                (hT_hi[:, f, part(c)], Wab_hi[:, f, :]), (hT_hi[:, f, part(c)], Wab_lo[:, f, :]),
                                (hT_lo[:, f, part(c)], Wab_hi[:, f, :]))]).then_inc(QV_ready, 1)

            run(pe, step, {-2: start, 0: w2_sums})


def kernel(x, adj, L0_gnn_W, L1_gnn_W1, L1_gnn_b1, L1_gnn_gamma, L1_gnn_beta, L1_gnn_W2, L1_gnn_b2):
    import numpy as np
    import concourse.bacc as bacc
    from concourse.bass_utils import run_bass_kernel_spmd

    x = np.ascontiguousarray(x)
    F = x.shape[2]
    W = np.asarray(L0_gnn_W)
    arrays = {
        "x": x,
        "adjT": np.ascontiguousarray(np.transpose(np.asarray(adj), (0, 2, 1))),
        "WabT": np.ascontiguousarray(W.reshape(W.shape[0], 2, F).transpose(2, 1, 0).reshape(F, -1)),
        "W1T": np.ascontiguousarray(np.asarray(L1_gnn_W1).T),
        "b1": np.ascontiguousarray(L1_gnn_b1),
        "gamma": np.ascontiguousarray(np.asarray(L1_gnn_gamma).reshape(-1, P).T),
        "beta": np.ascontiguousarray(np.asarray(L1_gnn_beta).reshape(-1, P).T),
        "W2T": np.ascontiguousarray(np.asarray(L1_gnn_W2).T),
        "b2": np.ascontiguousarray(L1_gnn_b2),
    }
    nc = bacc.Bacc("TRN2", target_bir_lowering=False, num_devices=1)
    args = [nc.dram_tensor(n, a.shape, mybir.dt.from_np(a.dtype), kind="ExternalInput").ap()
            for n, a in arrays.items()]
    args.append(nc.dram_tensor("out", x.shape, F32, kind="ExternalOutput").ap())
    gnn_two_layers_kernel(nc, *args)
    r = run_bass_kernel_spmd(nc, [arrays], core_ids=[0])
    return r.results[0]["out"]
```

```python
from contextlib import ExitStack

import concourse.bass as bass
from concourse import mybir

ALU = mybir.AluOpType
ACT = mybir.ActivationFunctionType
F32 = mybir.dt.float32
F32R = mybir.dt.float32r

P = 128
EPS_LN = 1e-5
EPS_DEG = 1e-6
TINY = 1.1754944e-38


class Graph:

    def __init__(self, round_, off, total):
        self.round, self.off, self.total = round_, off, total
        self.slot = off % 2
        self.exists = not isinstance(round_, int) or 0 <= off < total

    def plus(self, n):
        return Graph(self.round, self.off + n, self.total)

    def index(self):
        return self.round * 2 + self.off

    def count(self, per, part=None):
        return self.round * (2 * per) + (per * self.off + (per if part is None else part))

    def dma_count(self):
        return self.round * 16 + 16 * (self.off // 2 + 1)


def gnn_two_layers_kernel(nc, x, adjT, WabT, W1T, b1, gamma, beta, W2T, b2, out):
    B, N, F = x.shape
    O2 = WabT.shape[1]
    HID = W1T.shape[1]
    NC, HC = N // P, HID // P
    assert N == F == 2 * P and O2 == 2 * F and HID == 4 * P and B % 2 == 0

    x_v = x.rearrange("b (c p) f -> b p c f", p=P)
    adjT_v = adjT.rearrange("b (c p) n -> b p c n", p=P)
    out_v = out.rearrange("b (c p) f -> b p c f", p=P)

    with ExitStack() as ctx:
        def sb(name, shape, dt=F32):
            return ctx.enter_context(nc.sbuf_tensor(name, shape, dt))

        def sem(name):
            return ctx.enter_context(nc.semaphore(name))

        ident = sb("ident", [P, P])
        ones = sb("ones", [P, P])
        per_hidden = sb("per_hidden", [P, P])
        neg_half, neg_one, eps_ln = (sb(n, [P, NC]) for n in ("neg_half", "neg_one", "eps_ln"))
        WabT_raw = sb("WabT_raw", [P, NC, O2])
        W1T_raw = sb("W1T_raw", [P, NC, HID])
        W2T_raw = sb("W2T_raw", [P, HC, F])
        gamma_s = sb("gamma_s", [P, HC])
        beta_s = sb("beta_s", [P, HC])
        beta_bc = sb("beta_bc", [P, HC, P])
        W2g = sb("W2g", [P, HC, F])
        W2c = sb("W2c", [P, HC, F])
        Wab_hi, Wab_lo = sb("Wab_hi", [P, NC, O2], F32R), sb("Wab_lo", [P, NC, O2], F32R)
        W1_hi, W1_lo = sb("W1_hi", [P, NC, HID], F32R), sb("W1_lo", [P, NC, HID], F32R)
        W2_hi, W2_lo = sb("W2_hi", [P, HC, F], F32R), sb("W2_lo", [P, HC, F], F32R)
        b1_bc = sb("b1_bc", [P, HID])
        b2_bc = sb("b2_bc", [P, NC, F])
        cb_bc = sb("cb_bc", [P, F])

        x_s = [sb(f"x_s{i}", [P, NC, F]) for i in range(2)]
        adjT_s = [sb(f"adjT_s{i}", [P, NC, N]) for i in range(2)]
        adj_hi, adj_lo = sb("adj_hi", [P, NC, N], F32R), sb("adj_lo", [P, NC, N], F32R)
        stats1, mv1 = sb("stats1", [P, NC, 6]), sb("mv1", [P, NC, 2])
        ve1, nm1, rstd1 = sb("ve1", [P, NC]), sb("nm1", [P, NC]), sb("rstd1", [P, NC])
        z1 = sb("z1", [P, NC, F])
        hT_hi, hT_lo = sb("hT_hi", [P, NC, N], F32R), sb("hT_lo", [P, NC, N], F32R)
        V_hi, V_lo = sb("V_hi", [P, NC, F + 2], F32R), sb("V_lo", [P, NC, F], F32R)
        Q1 = sb("Q1", [P, NC, F])
        deg, rdeg = sb("deg", [P, NC]), sb("rdeg", [P, NC])
        agg = sb("agg", [P, NC, F])
        x1 = sb("x1", [P, NC, F])
        stats2, mv2 = sb("stats2", [P, NC, 6]), sb("mv2", [P, NC, 2])
        ve2, nm2, rstd2, nmr2 = (sb(n, [P, NC]) for n in ("ve2", "nm2", "rstd2", "nmr2"))
        h2 = sb("h2", [P, NC, F])
        h2_hi, h2_lo = sb("h2_hi", [P, NC, F], F32R), sb("h2_lo", [P, NC, F], F32R)
        HT = sb("HT", [P, NC, N], F32R)
        cnt, cnt1, Be, Be_lo = (sb(n, [P, NC]) for n in ("cnt", "cnt1", "Be", "Be_lo"))
        Be_hi = sb("Be_hi", [P, NC], F32R)
        B_hi, B_lo = sb("B_hi", [P, NC, N + 2], F32R), sb("B_lo", [P, NC, N + 2], F32R)
        A_hi = [sb(f"A_hi{i}", [P, NC, N], F32R) for i in range(2)]
        A_lo = [sb(f"A_lo{i}", [P, NC, N], F32R) for i in range(2)]
        D, Drec = sb("D", [P, NC]), sb("Drec", [P, NC])
        Dn = [sb(f"Dn{i}", [P, NC]) for i in range(2)]
        uT_hi, uT_lo = sb("uT_hi", [P, NC, N], F32R), sb("uT_lo", [P, NC, N], F32R)
        g = sb("g", [P, NC, HID])
        gsum, nmean3, var3 = (sb(n, [P, NC]) for n in ("gsum", "nmean3", "var3"))
        squares = sb("squares", [P, NC, HID])
        ve3, rstd3 = sb("ve3", [P, NC]), sb("rstd3", [P, NC])
        gT_hi, gT_lo = sb("gT_hi", [P, NC, HC, P], F32R), sb("gT_lo", [P, NC, HC, P], F32R)
        q = sb("q", [P, NC, F])
        q_hi, q_lo = sb("q_hi", [P, NC, F], F32R), sb("q_lo", [P, NC, F], F32R)
        y = [sb(f"y{i}", [P, NC, F]) for i in range(2)]

        bank = [ctx.enter_context(nc.psum_tensor(f"bank{i}", [P, 512], F32)) for i in range(8)]

        def chunks(t):
            return t[:, :].rearrange("p (c n) -> p c n", c=NC)

        ps_uT, ps_y, ps_T = chunks(bank[0]), chunks(bank[3]), chunks(bank[4])
        ps_q = [bank[6], bank[1]]
        ps_R = [bank[1], bank[2]]
        ps_w1 = [bank[5], bank[6]]
        ps_A = [bank[0], bank[7]]
        ps_QV = [bank[2], bank[5]]
        ps_gT = [bank[c][:, :].rearrange("p (o n) -> p o n", o=HC) for c in (3, 4)]
        ps_mean, ps_cb = bank[3], bank[6]

        wab_loaded, w1_loaded, w2_loaded, rows_loaded = map(sem, ("wab_loaded", "w1_loaded", "w2_loaded", "rows_loaded"))
        x_loaded = [sem(f"x_loaded{i}") for i in range(2)]
        adj_loaded = [sem(f"adj_loaded{i}") for i in range(2)]
        y_stored = [sem(f"y_stored{i}") for i in range(2)]
        names = ("const_zeroed const_ready "
                 "wab_hi_ready wab_ready w1_hi_ready w1_ready w2_scaled w2_sums_ready w2_centred w2_hi_ready w2_ready "
                 "T_ready QV_ready R_ready A_ready uT_ready w1out_ready gT_ready q_ready y_ready "
                 "adj_hi_ready QV_copied uT_hi_ready B_hi_ready g_ready hT_hi_ready gT_hi_ready A_hi_ready "
                 "h2_ready q_hi_ready "
                 "V_lo_ready stats1_ready mv1_ready uT_lo_ready HT_ready cnt1_ready Be_ready Be_hi_ready Be_lo_ready y_done conv1_ready "
                 "B_lo_ready nmean3_ready var3_ready deg_ready rdeg_ready agg_ready gT_lo_ready x1_ready "
                 "stats2_ready mv2_ready hT_lo_ready A_lo_ready Drec_ready Dn_ready h2_hi_ready qf_ready "
                 "adj_lo_ready w_lo_ready ve1_ready rstd1_ready z1_ready ve3_ready rstd3_ready ve2_ready rstd2_ready "
                 "norm2_ready x1b_ready h2_lo_ready q_lo_ready ypart_ready").split()
        s = {n: sem(n) for n in names}
        (const_zeroed, const_ready,
         wab_hi_ready, wab_ready, w1_hi_ready, w1_ready, w2_scaled, w2_sums_ready, w2_centred, w2_hi_ready, w2_ready,
         T_ready, QV_ready, R_ready, A_ready, uT_ready, w1out_ready, gT_ready, q_ready, y_ready,
         adj_hi_ready, QV_copied, uT_hi_ready, B_hi_ready, g_ready, hT_hi_ready, gT_hi_ready, A_hi_ready,
         h2_ready, q_hi_ready,
         V_lo_ready, stats1_ready, mv1_ready, uT_lo_ready, HT_ready, cnt1_ready, Be_ready, Be_hi_ready, Be_lo_ready, y_done, conv1_ready,
         B_lo_ready, nmean3_ready, var3_ready, deg_ready, rdeg_ready, agg_ready, gT_lo_ready, x1_ready,
         stats2_ready, mv2_ready, hT_lo_ready, A_lo_ready, Drec_ready, Dn_ready, h2_hi_ready, qf_ready,
         adj_lo_ready, w_lo_ready, ve1_ready, rstd1_ready, z1_ready, ve3_ready, rstd3_ready, ve2_ready, rstd2_ready,
         norm2_ready, x1b_ready, h2_lo_ready, q_lo_ready, ypart_ready) = (s[n] for n in names)

        LOOP_FROM, LOOP_ROUNDS = 1, (B - 4) // 2

        def run(eng, step, before=None):
            for b in range(-3, LOOP_FROM):
                if before and b in before:
                    before[b]()
                step(Graph(0, b, B))
            with eng.Fori(0, LOOP_ROUNDS) as r:
                for j in range(2):
                    step(Graph(r, LOOP_FROM + j, B))
            for b in range(LOOP_FROM + 2 * LOOP_ROUNDS, B + 1):
                step(Graph(0, b, B))

        block = ctx.enter_context(nc.Block())

        @block.sync
        def _(sp):
            def wab():
                sp.dma_start(WabT_raw[:, :, :], WabT.rearrange("(c p) o -> p c o", p=P)).then_inc(wab_loaded, 16)

            def more_weights():
                sp.dma_start(W1T_raw[:, :, :], W1T.rearrange("(c p) o -> p c o", p=P)).then_inc(w1_loaded, 16)
                sp.dma_start(W2T_raw[:, :, :], W2T.rearrange("(c p) o -> p c o", p=P)).then_inc(w2_loaded, 16)
                sp.dma_start(gamma_s[:, :], gamma).then_inc(rows_loaded, 16)
                sp.dma_start(beta_s[:, :], beta).then_inc(rows_loaded, 16)
                sp.dma_start(b1_bc[:, :], b1.partition_broadcast(P)).then_inc(rows_loaded, 16)
                for c in range(NC):
                    sp.dma_start(b2_bc[:, c, :], b2.partition_broadcast(P)).then_inc(rows_loaded, 16)

            def step(b):
                done, first, far = b.plus(-1), b.plus(1), b.plus(3)
                if far.exists:
                    if first.exists:
                        sp.wait_ge(x1_ready, first.count(1))
                    sp.dma_start(x_s[far.slot][:, :, :], x_v[far.index()]).then_inc(x_loaded[far.slot], 16)
                    if first.exists:
                        sp.wait_ge(w_lo_ready, first.count(1))
                    sp.dma_start(adjT_s[far.slot][:, :, :], adjT_v[far.index()]).then_inc(adj_loaded[far.slot], 16)
                if done.exists:
                    sp.wait_ge(y_done, done.count(1))
                    sp.dma_start(out_v[done.index()], y[done.slot][:, :, :]).then_inc(y_stored[done.slot], 16)

            run(sp, step, {-2: wab, -1: more_weights})
            for k in (B - 2, B - 1):
                sp.wait_ge(y_stored[k % 2], Graph(0, k, B).dma_count())

        @block.gpsimd
        def _(pool):
            def constants():
                pool.memset(ident[:, :], 0.0).then_inc(const_zeroed, 1)
                pool.memset(ones[:, :], 1.0)
                pool.memset(per_hidden[:, :], 1.0 / HID)
                pool.memset(neg_half[:, :], -0.5)
                pool.memset(neg_one[:, :], -1.0)
                pool.memset(eps_ln[:, :], EPS_LN)
                pool.memset(V_hi[:, :, F:F + 2].bitcast(F32), 1.0)
                pool.memset(B_hi[:, :, N:N + 2].bitcast(F32), 0.0)
                pool.memset(B_lo[:, :, N:N + 2].bitcast(F32), 0.0).then_inc(const_zeroed, 1)
                pool.wait_ge(const_zeroed, 2)
                pool.affine_select(out=ident[:, :], in_=ident[:, :], compare_op=ALU.not_equal, fill=1.0,
                                   base=0, pattern=[[-1, P]], channel_multiplier=1).then_inc(const_ready, 1)
                pool.wait_ge(const_ready, 1)

            def step(b):
                done, first, ahead, far = b.plus(-1), b.plus(1), b.plus(2), b.plus(3)
                if first.exists:
                    pool.wait_ge(B_hi_ready, first.count(1))
                    pool.tensor_tensor(B_lo[:, :, N:N + 1], adjT_s[first.slot][:, :, 0:1],
                                       B_hi[:, :, N:N + 1].bitcast(F32), ALU.subtract).then_inc(w_lo_ready, 1)
                if first.exists:
                    pool.wait_ge(mv2_ready, first.count(1))
                    pool.tensor_tensor(ve2[:, :], mv2[:, :, 1], eps_ln[:, :], ALU.add)
                    pool.tensor_tensor(nm2[:, :], mv2[:, :, 0], neg_one[:, :], ALU.mult).then_inc(ve2_ready, 1)
                    pool.wait_ge(ve2_ready, first.count(1))
                    pool.tensor_tensor(rstd2[:, :], ve2[:, :], neg_half[:, :], ALU.pow).then_inc(rstd2_ready, 1)
                    pool.wait_ge(rstd2_ready, first.count(1))
                    pool.tensor_tensor(nmr2[:, :], nm2[:, :], rstd2[:, :], ALU.mult).then_inc(norm2_ready, 1)
                if ahead.exists:
                    pool.wait_ge(adj_hi_ready, ahead.count(1))
                    pool.tensor_tensor(adj_lo[:, :, :], adjT_s[ahead.slot][:, :, :], adj_hi[:, :, :].bitcast(F32),
                                       ALU.subtract).then_inc(adj_lo_ready, 1)
                if first.exists:
                    if done.exists:
                        pool.wait_ge(y_stored[done.slot], done.dma_count())
                    if not b.exists:
                        pool.wait_ge(rows_loaded, 16 * (3 + NC))
                    pool.tensor_tensor(y[first.slot][:, :, :], x1[:, :, :], b2_bc[:, :, :],
                                       ALU.add).then_inc(x1b_ready, 1)
                    pool.wait_ge(x1b_ready, first.count(1))
                    pool.wait_ge(h2_ready, first.count(1))
                    pool.tensor_tensor(y[first.slot][:, :, :], y[first.slot][:, :, :], h2[:, :, :],
                                       ALU.add).then_inc(ypart_ready, 1)
                if far.exists:
                    pool.wait_ge(mv1_ready, far.count(1))
                    if ahead.exists:
                        pool.wait_ge(T_ready, ahead.count(1))
                    pool.tensor_tensor(ve1[:, :], mv1[:, :, 1], eps_ln[:, :], ALU.add)
                    pool.tensor_tensor(nm1[:, :], mv1[:, :, 0], neg_one[:, :], ALU.mult).then_inc(ve1_ready, 1)
                    pool.wait_ge(ve1_ready, far.count(1))
                    pool.tensor_tensor(rstd1[:, :], ve1[:, :], neg_half[:, :], ALU.pow).then_inc(rstd1_ready, 1)
                    pool.wait_ge(rstd1_ready, far.count(1))
                if first.exists:
                    pool.wait_ge(h2_hi_ready, first.count(1))
                    if b.exists:
                        pool.wait_ge(uT_ready, b.count(1))
                    pool.tensor_tensor(h2_lo[:, :, :], h2[:, :, :], h2_hi[:, :, :].bitcast(F32),
                                       ALU.subtract).then_inc(h2_lo_ready, 1)
                if b.exists:
                    pool.wait_ge(var3_ready, b.count(1))
                    pool.tensor_tensor(ve3[:, :], var3[:, :], eps_ln[:, :], ALU.add).then_inc(ve3_ready, 1)
                    pool.wait_ge(ve3_ready, b.count(1))
                    pool.tensor_tensor(rstd3[:, :], ve3[:, :], neg_half[:, :], ALU.pow).then_inc(rstd3_ready, 1)
                if far.exists:
                    for c in range(NC):
                        z = pool.tensor_scalar(z1[:, c, :], x_s[far.slot][:, c, :], nm1[:, c:c + 1],
                                               rstd1[:, c:c + 1], ALU.add, ALU.mult)
                    z.then_inc(z1_ready, 1)
                if b.exists:
                    for c in range(NC):
                        pool.wait_ge(q_hi_ready, b.count(NC, c + 1))
                        pool.tensor_tensor(q_lo[:, c, :], q[:, c, :], q_hi[:, c, :].bitcast(F32),
                                           ALU.subtract).then_inc(q_lo_ready, 1)

            run(pool, step, {-3: constants})

        @block.scalar
        def _(act):
            def wab():
                act.wait_ge(wab_loaded, 16)
                act.activation(Wab_hi[:, :, :], WabT_raw[:, :, :], ACT.Copy).then_inc(wab_hi_ready, 1)

            def w1():
                act.wait_ge(w1_loaded, 16)
                act.activation(W1_hi[:, :, :], W1T_raw[:, :, :], ACT.Copy).then_inc(w1_hi_ready, 1)

            def step(b):
                first, ahead = b.plus(1), b.plus(2)

                def copy_QV(c):
                    act.wait_ge(QV_ready, ahead.count(NC, c + 1))
                    if first.exists and c == 0:
                        act.wait_ge(agg_ready, first.count(1))
                    act.activation(V_hi[:, c, 0:F], ps_QV[c][:, F:2 * F], ACT.Copy)
                    act.activation(Q1[:, c, :], ps_QV[c][:, 0:F], ACT.Copy).then_inc(QV_copied, 1)

                if b.exists:
                    act.wait_ge(uT_ready, b.count(1))
                    act.activation(uT_hi[:, :, :], ps_uT, ACT.Copy).then_inc(uT_hi_ready, 1)
                if first.exists:
                    act.wait_ge(Be_ready, first.count(1))
                    act.activation(B_hi[:, :, N:N + 1], adjT_s[first.slot][:, :, 0:1], ACT.Copy)
                    for c in range(NC):
                        i = act.activation(B_hi[:, c, 0:N], HT[:, c, :].bitcast(F32), ACT.Copy, scale=Be[:, c:c + 1])
                    i.then_inc(B_hi_ready, 1)
                    act.wait_ge(Be_lo_ready, first.count(1))
                    for c in range(NC):
                        i = act.activation(B_lo[:, c, 0:N], HT[:, c, :].bitcast(F32), ACT.Copy,
                                           scale=Be_lo[:, c:c + 1])
                    i.then_inc(B_lo_ready, 1)
                if ahead.exists:
                    act.wait_ge(adj_loaded[ahead.slot], ahead.dma_count())
                    if first.exists:
                        act.wait_ge(R_ready, first.count(NC))
                    act.activation(adj_hi[:, :, :], adjT_s[ahead.slot][:, :, :], ACT.Copy).then_inc(adj_hi_ready, 1)
                    act.wait_ge(T_ready, ahead.count(1))
                    act.activation(hT_hi[:, :, :], ps_T, ACT.Relu).then_inc(hT_hi_ready, 1)
                if first.exists:
                    act.wait_ge(norm2_ready, first.count(1))
                    for c in range(NC):
                        i = act.activation(h2[:, c, :], x1[:, c, :], ACT.Relu, scale=rstd2[:, c:c + 1],
                                           bias=nmr2[:, c:c + 1])
                    i.then_inc(h2_ready, 1)
                if b.exists:
                    for c in range(NC):
                        act.wait_ge(conv1_ready, b.count(NC, c + 1))
                        act.activation(g[:, c, :], g[:, c, :], ACT.Relu, accum_out=gsum[:, c:c + 1]).then_inc(g_ready, 1)
                    act.wait_ge(g_ready, b.count(NC))
                    act.activation(nmean3[:, :], gsum[:, :], ACT.Copy,
                                   scale=-(HID ** -1.5)).then_inc(nmean3_ready, 1)
                if first.exists:
                    for c in range(NC):
                        act.wait_ge(A_ready, first.count(NC, c + 1))
                        act.activation(A_hi[first.slot][:, c, :], ps_A[c][:, 0:N], ACT.Copy).then_inc(A_hi_ready, 1)
                if ahead.exists:
                    copy_QV(0)
                if b.exists:
                    for c in range(NC):
                        act.wait_ge(gT_ready, b.count(NC, c + 1))
                        act.activation(gT_hi[:, c, :, :], ps_gT[c], ACT.Copy).then_inc(gT_hi_ready, 1)
                if first.exists:
                    act.wait_ge(h2_ready, first.count(1))
                    act.activation(h2_hi[:, :, :], h2[:, :, :], ACT.Copy).then_inc(h2_hi_ready, 1)
                if ahead.exists:
                    copy_QV(1)
                if b.exists:
                    act.wait_ge(nmean3_ready, b.count(1))
                    for c in range(NC):
                        i = act.activation(squares[:, c, :], g[:, c, :], ACT.Square, scale=HID ** -0.5,
                                           bias=nmean3[:, c:c + 1], accum_out=var3[:, c:c + 1])
                    i.then_inc(var3_ready, 1)
                if b.exists:
                    for c in range(NC):
                        act.wait_ge(qf_ready, b.count(NC, c + 1))
                        act.activation(q_hi[:, c, :], q[:, c, :], ACT.Copy).then_inc(q_hi_ready, 1)

            run(act, step, {-2: wab, -1: w1})

        @block.vector
        def _(dve):
            def wab():
                dve.wait_ge(wab_hi_ready, 1)
                dve.tensor_tensor(Wab_lo[:, :, :], WabT_raw[:, :, :], Wab_hi[:, :, :].bitcast(F32),
                                  ALU.subtract).then_inc(wab_ready, 1)

            def w1_w2():
                dve.wait_ge(w1_hi_ready, 1)
                dve.tensor_tensor(W1_lo[:, :, :], W1T_raw[:, :, :], W1_hi[:, :, :].bitcast(F32),
                                  ALU.subtract).then_inc(w1_ready, 1)
                dve.wait_ge(w2_loaded, 16)
                dve.wait_ge(rows_loaded, 16 * (3 + NC))
                dve.wait_ge(const_ready, 1)
                for o in range(HC):
                    dve.tensor_scalar(W2g[:, o, :], W2T_raw[:, o, :], gamma_s[:, o:o + 1], None, ALU.mult)
                    i = dve.tensor_scalar(beta_bc[:, o, :], ones[:, :], beta_s[:, o:o + 1], None, ALU.mult)
                i.then_inc(w2_scaled, 1)
                dve.wait_ge(w2_sums_ready, 1)
                for o in range(HC):
                    dve.tensor_tensor(W2c[:, o, :], W2g[:, o, :], ps_mean[:, 0:F], ALU.subtract)
                dve.tensor_copy(cb_bc[:, :], ps_cb[:, 0:F]).then_inc(w2_centred, 1)
                dve.wait_ge(w2_centred, 1)
                dve.tensor_copy(W2_hi[:, :, :], W2c[:, :, :]).then_inc(w2_hi_ready, 1)
                dve.wait_ge(w2_hi_ready, 1)
                dve.tensor_tensor(W2_lo[:, :, :], W2c[:, :, :], W2_hi[:, :, :].bitcast(F32),
                                  ALU.subtract).then_inc(w2_ready, 1)

            def step(b):
                done, first, ahead, far = b.plus(-1), b.plus(1), b.plus(2), b.plus(3)

                def low_half(ready, count, out_, whole, hi, lo_ready):
                    dve.wait_ge(ready, count)
                    dve.tensor_tensor(out_, whole, hi.bitcast(F32), ALU.subtract).then_inc(lo_ready, 1)

                def conv1(c):
                    dve.wait_ge(w1out_ready, b.count(NC, c + 1))
                    dve.scalar_tensor_tensor(out=g[:, c, :], in0=ps_w1[c][:, :], scalar=Dn[b.slot][:, c:c + 1],
                                             in1=b1_bc[:, :], op0=ALU.mult, op1=ALU.add).then_inc(conv1_ready, 1)

                if first.exists:
                    dve.wait_ge(adj_loaded[first.slot], first.dma_count())
                    if b.exists:
                        dve.wait_ge(A_ready, b.count(NC))
                    for c in range(NC):
                        i = dve.tensor_scalar(HT[:, c, :], adjT_s[first.slot][:, c, :], 0.0, None, ALU.not_equal,
                                              ALU.add, accum_out=cnt[:, c:c + 1])
                    i.then_inc(HT_ready, 1)
                    dve.wait_ge(HT_ready, first.count(1))
                    dve.tensor_scalar(cnt1[:, :], cnt[:, :], 1.0, None, ALU.max).then_inc(cnt1_ready, 1)
                    dve.wait_ge(cnt1_ready, first.count(1))
                    dve.reciprocal(Be[:, :], cnt1[:, :]).then_inc(Be_ready, 1)
                if b.exists:
                    low_half(uT_hi_ready, b.count(1), uT_lo[:, :, :], ps_uT, uT_hi[:, :, :], uT_lo_ready)
                if first.exists:
                    dve.wait_ge(Be_ready, first.count(1))
                    dve.tensor_copy(Be_hi[:, :], Be[:, :]).then_inc(Be_hi_ready, 1)
                    for c in range(NC):
                        dve.wait_ge(R_ready, first.count(NC, c + 1))
                        i = dve.tensor_scalar(deg[:, c:c + 1], ps_R[c][:, F:F + 1], EPS_DEG, None, ALU.max)
                    i.then_inc(deg_ready, 1)
                    dve.wait_ge(deg_ready, first.count(1))
                    dve.reciprocal(rdeg[:, :], deg[:, :]).then_inc(rdeg_ready, 1)
                    dve.wait_ge(rdeg_ready, first.count(1))
                    for c in range(NC):
                        i = dve.scalar_tensor_tensor(out=agg[:, c, :], in0=ps_R[c][:, 0:F], scalar=rdeg[:, c:c + 1],
                                                     in1=Q1[:, c, :], op0=ALU.mult, op1=ALU.add)
                    i.then_inc(agg_ready, 1)
                    dve.wait_ge(agg_ready, first.count(1))
                    dve.scalar_tensor_tensor(out=x1[:, :, :], in0=agg[:, :, :], scalar=0.0,
                                             in1=x_s[first.slot][:, :, :], op0=ALU.max,
                                             op1=ALU.add).then_inc(x1_ready, 1)
                    dve.wait_ge(x1_ready, first.count(1))
                    for c in range(NC):
                        i = dve.bn_stats(stats2[:, c, :], x1[:, c, :])
                    i.then_inc(stats2_ready, 1)
                    dve.wait_ge(stats2_ready, first.count(1))
                    dve.wait_ge(Be_hi_ready, first.count(1))
                    dve.tensor_tensor(Be_lo[:, :], Be[:, :], Be_hi[:, :].bitcast(F32),
                                      ALU.subtract).then_inc(Be_lo_ready, 1)
                    for c in range(NC):
                        i = dve.bn_aggr(mv2[:, c, :], stats2[:, c, :])
                    i.then_inc(mv2_ready, 1)
                if ahead.exists:
                    dve.wait_ge(hT_hi_ready, ahead.count(1))
                    dve.scalar_tensor_tensor(out=hT_lo[:, :, :], in0=ps_T, scalar=0.0, in1=hT_hi[:, :, :].bitcast(F32),
                                             op0=ALU.max, op1=ALU.subtract).then_inc(hT_lo_ready, 1)
                if done.exists:
                    dve.wait_ge(y_ready, done.count(1))
                    dve.wait_ge(ypart_ready, done.count(1))
                    for c in range(NC):
                        i = dve.scalar_tensor_tensor(out=y[done.slot][:, c, :], in0=ps_y[:, c, :],
                                                     scalar=Dn[done.slot][:, c:c + 1], in1=y[done.slot][:, c, :],
                                                     op0=ALU.mult, op1=ALU.add)
                    i.then_inc(y_done, 1)
                if b.exists:
                    dve.wait_ge(Dn_ready, b.count(1))
                    for c in range(NC):
                        conv1(c)
                if far.exists:
                    dve.wait_ge(x_loaded[far.slot], far.dma_count())
                    for c in range(NC):
                        i = dve.bn_stats(stats1[:, c, :], x_s[far.slot][:, c, :])
                    i.then_inc(stats1_ready, 1)
                    dve.wait_ge(stats1_ready, far.count(1))
                if first.exists:
                    for c in range(NC):
                        dve.wait_ge(A_hi_ready, first.count(NC, c + 1))
                        dve.tensor_scalar(D[:, c:c + 1], ps_A[c][:, N:N + 1], TINY, None, ALU.max)
                        dve.tensor_tensor(A_lo[first.slot][:, c, :], ps_A[c][:, 0:N],
                                          A_hi[first.slot][:, c, :].bitcast(F32), ALU.subtract).then_inc(A_lo_ready, 1)
                if far.exists:
                    for c in range(NC):
                        i = dve.bn_aggr(mv1[:, c, :], stats1[:, c, :])
                    i.then_inc(mv1_ready, 1)
                if first.exists:
                    dve.wait_ge(A_lo_ready, first.count(NC))
                    dve.reciprocal(Drec[:, :], D[:, :]).then_inc(Drec_ready, 1)
                if ahead.exists:
                    low_half(QV_copied, ahead.count(NC, 1), V_lo[:, 0, :], ps_QV[0][:, F:2 * F], V_hi[:, 0, 0:F],
                             V_lo_ready)
                if first.exists:
                    dve.wait_ge(Drec_ready, first.count(1))
                    dve.scalar_tensor_tensor(out=Dn[first.slot][:, :], in0=D[:, :], scalar=TINY, in1=Drec[:, :],
                                             op0=ALU.is_gt, op1=ALU.mult).then_inc(Dn_ready, 1)
                if b.exists:
                    for c in range(NC):
                        low_half(gT_hi_ready, b.count(NC, c + 1), gT_lo[:, c, :, :], ps_gT[c], gT_hi[:, c, :, :],
                                 gT_lo_ready)
                if ahead.exists:
                    low_half(QV_copied, ahead.count(NC, 2), V_lo[:, 1, :], ps_QV[1][:, F:2 * F], V_hi[:, 1, 0:F],
                             V_lo_ready)
                if b.exists:
                    dve.wait_ge(rstd3_ready, b.count(1))
                    for c in range(NC):
                        dve.wait_ge(q_ready, b.count(NC, c + 1))
                        dve.scalar_tensor_tensor(out=q[:, c, :], in0=ps_q[c][:, 0:F], scalar=rstd3[:, c:c + 1],
                                                 in1=cb_bc[:, :], op0=ALU.mult, op1=ALU.add).then_inc(qf_ready, 1)

            run(dve, step, {-2: wab, 0: w1_w2})

        @block.tensor
        def _(pe):
            def product(out_, pairs):
                for n, (lhsT, rhs) in enumerate(pairs):
                    i = pe.matmul(out_[:, 0:rhs.shape[-1]], lhsT, rhs, start=n == 0, stop=n == len(pairs) - 1)
                return i

            def three(lhs_hi, lhs_lo, rhs_hi, rhs_lo):
                return [pair for k in range(NC)
                        for pair in ((lhs_hi(k), rhs_hi(k)), (lhs_hi(k), rhs_lo(k)), (lhs_lo(k), rhs_hi(k)))]

            def part(c):
                return slice(c * P, (c + 1) * P)

            def w2_sums():
                pe.wait_ge(w2_scaled, 1)
                product(ps_mean, [(per_hidden[:, :], W2g[:, o, :]) for o in range(HC)])
                product(ps_cb, [(beta_bc[:, o, :], W2T_raw[:, o, :]) for o in range(HC)]).then_inc(w2_sums_ready, 1)

            def start():
                pe.wait_ge(const_ready, 1)

            def step(b):
                done, first, ahead = b.plus(-1), b.plus(1), b.plus(2)

                def QV(c):
                    product(ps_QV[c], three(
                        lambda f: hT_hi[:, f, part(c)], lambda f: hT_lo[:, f, part(c)],
                        lambda f: Wab_hi[:, f, :], lambda f: Wab_lo[:, f, :])).then_inc(QV_ready, 1)

                if b.exists:
                    pe.wait_ge(h2_lo_ready, b.count(1))
                    pe.wait_ge(A_lo_ready, b.count(NC))
                    for f in range(NC):
                        i = product(ps_uT[:, f, :], three(
                            lambda k: h2_hi[:, k, part(f)], lambda k: h2_lo[:, k, part(f)],
                            lambda k: A_hi[b.slot][:, k, :], lambda k: A_lo[b.slot][:, k, :]))
                    i.then_inc(uT_ready, 1)
                if first.exists:
                    pe.wait_ge(V_lo_ready, first.count(NC))
                    pe.wait_ge(adj_lo_ready, first.count(1))
                    if done.exists:
                        pe.wait_ge(qf_ready, done.count(NC))
                    for c in range(NC):
                        product(ps_R[c], three(
                            lambda k: adj_hi[:, k, part(c)], lambda k: adj_lo[:, k, part(c)],
                            lambda k: V_hi[:, k, :], lambda k: V_lo[:, k, :])).then_inc(R_ready, 1)
                if done.exists:
                    pe.wait_ge(q_lo_ready, done.count(NC))
                    for c in range(NC):
                        i = product(ps_y[:, c, :], three(
                            lambda k: A_hi[done.slot][:, k, part(c)], lambda k: A_lo[done.slot][:, k, part(c)],
                            lambda k: q_hi[:, k, :], lambda k: q_lo[:, k, :]))
                    i.then_inc(y_ready, 1)
                if ahead.exists:
                    pe.wait_ge(z1_ready, ahead.count(1))
                    for f in range(NC):
                        for c in range(NC):
                            i = pe.transpose(ps_T[:, f, part(c)], z1[:, c, part(f)], ident[:, :])
                    i.then_inc(T_ready, 1)
                if b.exists:
                    pe.wait_ge(uT_lo_ready, b.count(1))
                    if not done.exists:
                        pe.wait_ge(w2_centred, 1)
                        pe.wait_ge(w1_ready, 1)
                    for c in range(NC):
                        product(ps_w1[c], three(
                            lambda f: uT_hi[:, f, part(c)], lambda f: uT_lo[:, f, part(c)],
                            lambda f: W1_hi[:, f, :], lambda f: W1_lo[:, f, :])).then_inc(w1out_ready, 1)
                if first.exists:
                    pe.wait_ge(B_lo_ready, first.count(1))
                    pe.wait_ge(w_lo_ready, first.count(1))
                    for c in range(NC):
                        product(ps_A[c], [
                            pair for e in range(NC) for pair in (
                                (HT[:, e, part(c)], B_hi[:, e, :]), (HT[:, e, part(c)], B_lo[:, e, :]))]
                                ).then_inc(A_ready, 1)
                if ahead.exists:
                    pe.wait_ge(hT_lo_ready, ahead.count(1))
                    if first.exists:
                        pe.wait_ge(agg_ready, first.count(1))
                    else:
                        pe.wait_ge(wab_ready, 1)
                    QV(0)
                if b.exists:
                    if done.exists:
                        pe.wait_ge(y_done, done.count(1))
                    for c in range(NC):
                        pe.wait_ge(g_ready, b.count(NC, c + 1))
                        for o in range(HC):
                            i = pe.transpose(ps_gT[c][:, o, :], g[:, c, part(o)], ident[:, :])
                        i.then_inc(gT_ready, 1)
                if ahead.exists:
                    QV(1)
                if b.exists:
                    if not done.exists:
                        pe.wait_ge(w2_ready, 1)
                    if first.exists:
                        pe.wait_ge(agg_ready, first.count(1))
                    for c in range(NC):
                        pe.wait_ge(gT_lo_ready, b.count(NC, c + 1))
                        product(ps_q[c], [
                            pair for o in range(HC) for pair in (
                                (gT_hi[:, c, o, :], W2_hi[:, o, :]), (gT_hi[:, c, o, :], W2_lo[:, o, :]),
                                (gT_lo[:, c, o, :], W2_hi[:, o, :]))]).then_inc(q_ready, 1)

            run(pe, step, {-3: start, 0: w2_sums})


def kernel(x, adj, L0_gnn_W, L1_gnn_W1, L1_gnn_b1, L1_gnn_gamma, L1_gnn_beta, L1_gnn_W2, L1_gnn_b2):
    import numpy as np
    import concourse.bacc as bacc
    from concourse.bass_utils import run_bass_kernel_spmd

    x = np.ascontiguousarray(x)
    F = x.shape[2]
    W = np.asarray(L0_gnn_W)
    arrays = {
        "x": x,
        "adjT": np.ascontiguousarray(np.transpose(np.asarray(adj), (0, 2, 1))),
        "WabT": np.ascontiguousarray(W.reshape(W.shape[0], 2, F).transpose(2, 1, 0).reshape(F, -1)),
        "W1T": np.ascontiguousarray(np.asarray(L1_gnn_W1).T),
        "b1": np.ascontiguousarray(L1_gnn_b1),
        "gamma": np.ascontiguousarray(np.asarray(L1_gnn_gamma).reshape(-1, P).T),
        "beta": np.ascontiguousarray(np.asarray(L1_gnn_beta).reshape(-1, P).T),
        "W2T": np.ascontiguousarray(np.asarray(L1_gnn_W2).T),
        "b2": np.ascontiguousarray(L1_gnn_b2),
    }
    nc = bacc.Bacc("TRN2", target_bir_lowering=False, num_devices=1)
    args = [nc.dram_tensor(n, a.shape, mybir.dt.from_np(a.dtype), kind="ExternalInput").ap()
            for n, a in arrays.items()]
    args.append(nc.dram_tensor("out", x.shape, F32, kind="ExternalOutput").ap())
    gnn_two_layers_kernel(nc, *args)
    r = run_bass_kernel_spmd(nc, [arrays], core_ids=[0])
    return r.results[0]["out"]
```

```python
from contextlib import ExitStack

import concourse.bass as bass
from concourse import mybir

ALU = mybir.AluOpType
ACT = mybir.ActivationFunctionType
F32 = mybir.dt.float32
F32R = mybir.dt.float32r

P = 128
EPS_LN = 1e-5
EPS_DEG = 1e-6
WARM_UP = 24
TINY = 1.1754944e-38


class Graph:

    def __init__(self, round_, off, total):
        self.round, self.off, self.total = round_, off, total
        self.slot = off % 2
        self.exists = not isinstance(round_, int) or 0 <= off < total

    def plus(self, n):
        return Graph(self.round, self.off + n, self.total)

    def index(self):
        return self.round * 2 + self.off

    def count(self, per, part=None):
        return self.round * (2 * per) + (per * self.off + (per if part is None else part))

    def dma_count(self):
        return self.round * 16 + 16 * (self.off // 2 + 1)


def gnn_two_layers_kernel(nc, x, adjT, WabT, W1T, b1, gamma, beta, W2T, b2, out):
    B, N, F = x.shape
    O2 = WabT.shape[1]
    HID = W1T.shape[1]
    NC, HC = N // P, HID // P
    assert N == F == 2 * P and O2 == 2 * F and HID == 4 * P and B % 2 == 0

    x_v = x.rearrange("b (c p) f -> b p c f", p=P)
    adjT_v = adjT.rearrange("b (c p) n -> b p c n", p=P)
    out_v = out.rearrange("b (c p) f -> b p c f", p=P)

    with ExitStack() as ctx:
        def sb(name, shape, dt=F32):
            return ctx.enter_context(nc.sbuf_tensor(name, shape, dt))

        def sem(name):
            return ctx.enter_context(nc.semaphore(name))

        ident = sb("ident", [P, P])
        ones = sb("ones", [P, P])
        per_hidden = sb("per_hidden", [P, P])
        neg_half, neg_one, eps_ln = (sb(n, [P, NC]) for n in ("neg_half", "neg_one", "eps_ln"))
        WabT_raw = sb("WabT_raw", [P, NC, O2])
        W1T_raw = sb("W1T_raw", [P, NC, HID])
        W2T_raw = sb("W2T_raw", [P, HC, F])
        gamma_s = sb("gamma_s", [P, HC])
        beta_s = sb("beta_s", [P, HC])
        beta_bc = sb("beta_bc", [P, HC, P])
        W2g = sb("W2g", [P, HC, F])
        W2c = sb("W2c", [P, HC, F])
        Wab_hi, Wab_lo = sb("Wab_hi", [P, NC, O2], F32R), sb("Wab_lo", [P, NC, O2], F32R)
        W1_hi, W1_lo = sb("W1_hi", [P, NC, HID], F32R), sb("W1_lo", [P, NC, HID], F32R)
        W2_hi, W2_lo = sb("W2_hi", [P, HC, F], F32R), sb("W2_lo", [P, HC, F], F32R)
        b1_bc = sb("b1_bc", [P, HID])
        b2_bc = sb("b2_bc", [P, NC, F])
        cb_bc = sb("cb_bc", [P, F])

        x_s = [sb(f"x_s{i}", [P, NC, F]) for i in range(2)]
        adjT_s = [sb(f"adjT_s{i}", [P, NC, N]) for i in range(2)]
        adj_hi, adj_lo = sb("adj_hi", [P, NC, N], F32R), sb("adj_lo", [P, NC, N], F32R)
        stats1, mv1 = sb("stats1", [P, NC, 6]), sb("mv1", [P, NC, 2])
        ve1, nm1, rstd1 = sb("ve1", [P, NC]), sb("nm1", [P, NC]), sb("rstd1", [P, NC])
        z1 = sb("z1", [P, NC, F])
        hT_hi, hT_lo = sb("hT_hi", [P, NC, N], F32R), sb("hT_lo", [P, NC, N], F32R)
        V_hi, V_lo = sb("V_hi", [P, NC, F + 2], F32R), sb("V_lo", [P, NC, F], F32R)
        Q1 = sb("Q1", [P, NC, F])
        deg, rdeg = sb("deg", [P, NC]), sb("rdeg", [P, NC])
        agg = sb("agg", [P, NC, F])
        x1 = sb("x1", [P, NC, F])
        stats2, mv2 = sb("stats2", [P, NC, 6]), sb("mv2", [P, NC, 2])
        ve2, nm2, rstd2, nmr2 = (sb(n, [P, NC]) for n in ("ve2", "nm2", "rstd2", "nmr2"))
        h2 = sb("h2", [P, NC, F])
        h2_hi, h2_lo = sb("h2_hi", [P, NC, F], F32R), sb("h2_lo", [P, NC, F], F32R)
        HT = sb("HT", [P, NC, N], F32R)
        cnt, cnt1, Be, Be_lo = (sb(n, [P, NC]) for n in ("cnt", "cnt1", "Be", "Be_lo"))
        Be_hi = sb("Be_hi", [P, NC], F32R)
        B_hi, B_lo = sb("B_hi", [P, NC, N + 2], F32R), sb("B_lo", [P, NC, N + 2], F32R)
        A_hi = [sb(f"A_hi{i}", [P, NC, N], F32R) for i in range(2)]
        A_lo = [sb(f"A_lo{i}", [P, NC, N], F32R) for i in range(2)]
        D, Drec = sb("D", [P, NC]), sb("Drec", [P, NC])
        Dn = [sb(f"Dn{i}", [P, NC]) for i in range(2)]
        uT_hi, uT_lo = sb("uT_hi", [P, NC, N], F32R), sb("uT_lo", [P, NC, N], F32R)
        g = sb("g", [P, NC, HID])
        gsum, nmean3, var3 = (sb(n, [P, NC]) for n in ("gsum", "nmean3", "var3"))
        squares = sb("squares", [P, NC, HID])
        ve3, rstd3 = sb("ve3", [P, NC]), sb("rstd3", [P, NC])
        gT_hi, gT_lo = sb("gT_hi", [P, NC, HC, P], F32R), sb("gT_lo", [P, NC, HC, P], F32R)
        q = sb("q", [P, NC, F])
        q_hi, q_lo = sb("q_hi", [P, NC, F], F32R), sb("q_lo", [P, NC, F], F32R)
        y = [sb(f"y{i}", [P, NC, F]) for i in range(2)]

        bank = [ctx.enter_context(nc.psum_tensor(f"bank{i}", [P, 512], F32)) for i in range(8)]

        def chunks(t):
            return t[:, :].rearrange("p (c n) -> p c n", c=NC)

        ps_uT, ps_T, ps_y = chunks(bank[0]), chunks(bank[3]), chunks(bank[5])
        ps_R = [bank[1], bank[2]]
        ps_A = [bank[4], bank[7]]
        ps_w1 = [bank[5], bank[6]]
        ps_gT = [bank[c][:, :].rearrange("p (o n) -> p o n", o=HC) for c in (0, 1)]
        ps_QV = [bank[2], bank[3]]
        ps_q = [bank[7], bank[6]]
        ps_mean, ps_cb = bank[5], bank[6]

        wab_loaded, w1_loaded, w2_loaded, rows_loaded = map(sem, ("wab_loaded", "w1_loaded", "w2_loaded", "rows_loaded"))
        x_loaded = [sem(f"x_loaded{i}") for i in range(2)]
        adj_loaded = [sem(f"adj_loaded{i}") for i in range(2)]
        y_stored = [sem(f"y_stored{i}") for i in range(2)]
        names = ("const_zeroed const_ready "
                 "wab_hi_ready wab_ready w1_hi_ready w1_ready w2_scaled w2_sums_ready w2_centred w2_hi_ready w2_ready "
                 "T_ready QV_ready R_ready A_ready uT_ready w1out_ready gT_ready q_ready y_ready "
                 "adj_hi_ready QV_copied uT_hi_ready B_hi_ready g_ready hT_hi_ready gT_hi_ready A_hi_ready "
                 "h2_ready q_hi_ready "
                 "V_lo_ready stats1_ready mv1_ready uT_lo_ready HT_ready cnt1_ready Be_ready Be_hi_ready Be_lo_ready y_done conv1_ready "
                 "B_lo_ready nmean3_ready var3_ready deg_ready rdeg_ready agg_ready gT_lo_ready x1_ready "
                 "stats2_ready mv2_ready hT_lo_ready A_lo_ready Drec_ready Dn_ready h2_hi_ready qf_ready "
                 "adj_lo_ready w_lo_ready ve1_ready rstd1_ready z1_ready ve3_ready rstd3_ready ve2_ready rstd2_ready "
                 "norm2_ready x1b_ready h2_lo_ready q_lo_ready ypart_ready").split()
        s = {n: sem(n) for n in names}
        (const_zeroed, const_ready,
         wab_hi_ready, wab_ready, w1_hi_ready, w1_ready, w2_scaled, w2_sums_ready, w2_centred, w2_hi_ready, w2_ready,
         T_ready, QV_ready, R_ready, A_ready, uT_ready, w1out_ready, gT_ready, q_ready, y_ready,
         adj_hi_ready, QV_copied, uT_hi_ready, B_hi_ready, g_ready, hT_hi_ready, gT_hi_ready, A_hi_ready,
         h2_ready, q_hi_ready,
         V_lo_ready, stats1_ready, mv1_ready, uT_lo_ready, HT_ready, cnt1_ready, Be_ready, Be_hi_ready, Be_lo_ready, y_done, conv1_ready,
         B_lo_ready, nmean3_ready, var3_ready, deg_ready, rdeg_ready, agg_ready, gT_lo_ready, x1_ready,
         stats2_ready, mv2_ready, hT_lo_ready, A_lo_ready, Drec_ready, Dn_ready, h2_hi_ready, qf_ready,
         adj_lo_ready, w_lo_ready, ve1_ready, rstd1_ready, z1_ready, ve3_ready, rstd3_ready, ve2_ready, rstd2_ready,
         norm2_ready, x1b_ready, h2_lo_ready, q_lo_ready, ypart_ready) = (s[n] for n in names)

        LOOP_FROM, LOOP_ROUNDS = 1, (B - 4) // 2

        def run(eng, step, before=None):
            for b in range(-3, LOOP_FROM):
                if before and b in before:
                    before[b]()
                step(Graph(0, b, B))
            with eng.Fori(0, LOOP_ROUNDS) as r:
                for j in range(2):
                    step(Graph(r, LOOP_FROM + j, B))
            for b in range(LOOP_FROM + 2 * LOOP_ROUNDS, B + 1):
                step(Graph(0, b, B))

        block = ctx.enter_context(nc.Block())

        @block.sync
        def _(sp):
            def wab():
                sp.dma_start(WabT_raw[:, :, :], WabT.rearrange("(c p) o -> p c o", p=P)).then_inc(wab_loaded, 16)

            def w1_w2():
                sp.dma_start(W1T_raw[:, :, :], W1T.rearrange("(c p) o -> p c o", p=P)).then_inc(w1_loaded, 16)
                sp.dma_start(W2T_raw[:, :, :], W2T.rearrange("(c p) o -> p c o", p=P)).then_inc(w2_loaded, 16)
                sp.dma_start(gamma_s[:, :], gamma).then_inc(rows_loaded, 16)
                sp.dma_start(beta_s[:, :], beta).then_inc(rows_loaded, 16)
                sp.dma_start(b1_bc[:, :], b1.partition_broadcast(P)).then_inc(rows_loaded, 16)
                for c in range(NC):
                    sp.dma_start(b2_bc[:, c, :], b2.partition_broadcast(P)).then_inc(rows_loaded, 16)

            def step(b):
                done, first, far = b.plus(-1), b.plus(1), b.plus(3)
                if far.exists:
                    if first.exists:
                        sp.wait_ge(x1_ready, first.count(1))
                    sp.dma_start(x_s[far.slot][:, :, :], x_v[far.index()]).then_inc(x_loaded[far.slot], 16)
                    if first.exists:
                        sp.wait_ge(w_lo_ready, first.count(1))
                    sp.dma_start(adjT_s[far.slot][:, :, :], adjT_v[far.index()]).then_inc(adj_loaded[far.slot], 16)
                if done.exists:
                    sp.wait_ge(y_done, done.count(1))
                    sp.dma_start(out_v[done.index()], y[done.slot][:, :, :]).then_inc(y_stored[done.slot], 16)

            run(sp, step, {-2: wab, -1: w1_w2})
            for k in (B - 2, B - 1):
                sp.wait_ge(y_stored[k % 2], Graph(0, k, B).dma_count())

        @block.gpsimd
        def _(pool):
            def constants():
                pool.memset(ident[:, :], 0.0).then_inc(const_zeroed, 1)
                pool.memset(ones[:, :], 1.0)
                pool.memset(per_hidden[:, :], 1.0 / HID)
                pool.memset(neg_half[:, :], -0.5)
                pool.memset(neg_one[:, :], -1.0)
                pool.memset(eps_ln[:, :], EPS_LN)
                pool.memset(V_hi[:, :, F:F + 2].bitcast(F32), 1.0)
                pool.memset(B_hi[:, :, N:N + 2].bitcast(F32), 0.0)
                pool.memset(B_lo[:, :, N:N + 2].bitcast(F32), 0.0).then_inc(const_zeroed, 1)
                pool.wait_ge(const_zeroed, 2)
                pool.affine_select(out=ident[:, :], in_=ident[:, :], compare_op=ALU.not_equal, fill=1.0,
                                   base=0, pattern=[[-1, P]], channel_multiplier=1).then_inc(const_ready, 1)
                pool.wait_ge(const_ready, 1)

            def w1_low():
                pool.wait_ge(w1_hi_ready, 1)
                pool.tensor_tensor(W1_lo[:, :, :], W1T_raw[:, :, :], W1_hi[:, :, :].bitcast(F32),
                                   ALU.subtract).then_inc(w1_ready, 1)

            def w2_low():
                pool.wait_ge(w2_hi_ready, 1)
                pool.tensor_tensor(W2_lo[:, :, :], W2c[:, :, :], W2_hi[:, :, :].bitcast(F32),
                                   ALU.subtract).then_inc(w2_ready, 1)

            def step(b):
                done, first, ahead, far = b.plus(-1), b.plus(1), b.plus(2), b.plus(3)
                if done.exists:
                    for c in range(NC):
                        pool.wait_ge(q_hi_ready, done.count(NC, c + 1))
                        pool.tensor_tensor(q_lo[:, c, :], q[:, c, :], q_hi[:, c, :].bitcast(F32),
                                           ALU.subtract).then_inc(q_lo_ready, 1)
                if first.exists:
                    pool.wait_ge(mv2_ready, first.count(1))
                    pool.tensor_tensor(ve2[:, :], mv2[:, :, 1], eps_ln[:, :], ALU.add)
                    pool.tensor_tensor(nm2[:, :], mv2[:, :, 0], neg_one[:, :], ALU.mult).then_inc(ve2_ready, 1)
                    pool.wait_ge(ve2_ready, first.count(1))
                    pool.tensor_tensor(rstd2[:, :], ve2[:, :], neg_half[:, :], ALU.pow).then_inc(rstd2_ready, 1)
                    pool.wait_ge(rstd2_ready, first.count(1))
                    pool.tensor_tensor(nmr2[:, :], nm2[:, :], rstd2[:, :], ALU.mult).then_inc(norm2_ready, 1)
                if ahead.exists:
                    pool.wait_ge(adj_hi_ready, ahead.count(1))
                    pool.tensor_tensor(adj_lo[:, :, :], adjT_s[ahead.slot][:, :, :], adj_hi[:, :, :].bitcast(F32),
                                       ALU.subtract).then_inc(adj_lo_ready, 1)
                if first.exists and not b.exists:
                    w1_low()
                if far.exists:
                    pool.wait_ge(mv1_ready, far.count(1))
                    pool.tensor_tensor(ve1[:, :], mv1[:, :, 1], eps_ln[:, :], ALU.add)
                    pool.tensor_tensor(nm1[:, :], mv1[:, :, 0], neg_one[:, :], ALU.mult).then_inc(ve1_ready, 1)
                    pool.wait_ge(ve1_ready, far.count(1))
                    pool.tensor_tensor(rstd1[:, :], ve1[:, :], neg_half[:, :], ALU.pow).then_inc(rstd1_ready, 1)
                if b.exists:
                    pool.wait_ge(var3_ready, b.count(1))
                    pool.tensor_tensor(ve3[:, :], var3[:, :], eps_ln[:, :], ALU.add).then_inc(ve3_ready, 1)
                    pool.wait_ge(ve3_ready, b.count(1))
                    pool.tensor_tensor(rstd3[:, :], ve3[:, :], neg_half[:, :], ALU.pow).then_inc(rstd3_ready, 1)
                if ahead.exists:
                    pool.wait_ge(B_hi_ready, ahead.count(1))
                    pool.tensor_tensor(B_lo[:, :, N:N + 1], adjT_s[ahead.slot][:, :, 0:1],
                                       B_hi[:, :, N:N + 1].bitcast(F32), ALU.subtract).then_inc(w_lo_ready, 1)
                if first.exists:
                    pool.wait_ge(x1_ready, first.count(1))
                    if done.exists:
                        pool.wait_ge(y_stored[done.slot], done.dma_count())
                    if not b.exists:
                        pool.wait_ge(rows_loaded, 16 * (3 + NC))
                    pool.tensor_tensor(y[first.slot][:, :, :], x1[:, :, :], b2_bc[:, :, :],
                                       ALU.add).then_inc(x1b_ready, 1)
                    pool.wait_ge(x1b_ready, first.count(1))
                    pool.wait_ge(h2_ready, first.count(1))
                    pool.tensor_tensor(y[first.slot][:, :, :], y[first.slot][:, :, :], h2[:, :, :],
                                       ALU.add).then_inc(ypart_ready, 1)

            run(pool, step, {-3: constants, 0: w2_low})

        @block.scalar
        def _(act):
            def wab():
                act.wait_ge(wab_loaded, 16)
                act.activation(Wab_hi[:, :, :], WabT_raw[:, :, :], ACT.Copy).then_inc(wab_hi_ready, 1)

            def w1_hi_and_w2_scale():
                act.wait_ge(w2_loaded, 16)
                act.wait_ge(rows_loaded, 16 * (3 + NC))
                act.wait_ge(const_ready, 1)
                for o in range(HC):
                    act.activation(W2g[:, o, :], W2T_raw[:, o, :], ACT.Copy, scale=gamma_s[:, o:o + 1])
                    i = act.activation(beta_bc[:, o, :], ones[:, :], ACT.Copy, scale=beta_s[:, o:o + 1])
                i.then_inc(w2_scaled, 1)
                act.wait_ge(w1_loaded, 16)
                act.activation(W1_hi[:, :, :], W1T_raw[:, :, :], ACT.Copy).then_inc(w1_hi_ready, 1)

            def w2_hi():
                act.wait_ge(w2_centred, 1)
                act.activation(W2_hi[:, :, :], W2c[:, :, :], ACT.Copy).then_inc(w2_hi_ready, 1)

            def step(b):
                done, first, ahead = b.plus(-1), b.plus(1), b.plus(2)

                def copy_QV(c):
                    act.wait_ge(QV_ready, ahead.count(NC, c + 1))
                    act.activation(V_hi[:, c, 0:F], ps_QV[c][:, F:2 * F], ACT.Copy)
                    act.activation(Q1[:, c, :], ps_QV[c][:, 0:F], ACT.Copy).then_inc(QV_copied, 1)

                def copy_A(c):
                    act.wait_ge(A_ready, first.count(NC, c + 1))
                    act.activation(A_hi[first.slot][:, c, :], ps_A[c][:, 0:N], ACT.Copy).then_inc(A_hi_ready, 1)

                def copy_gT(c):
                    act.wait_ge(gT_ready, b.count(NC, c + 1))
                    act.activation(gT_hi[:, c, :, :], ps_gT[c], ACT.Copy).then_inc(gT_hi_ready, 1)

                if b.exists:
                    act.wait_ge(uT_ready, b.count(1))
                    act.activation(uT_hi[:, :, :], ps_uT, ACT.Copy).then_inc(uT_hi_ready, 1)
                if first.exists:
                    act.wait_ge(Be_lo_ready, first.count(1))
                    for c in range(NC):
                        i = act.activation(B_lo[:, c, 0:N], HT[:, c, :].bitcast(F32), ACT.Copy,
                                           scale=Be_lo[:, c:c + 1])
                    i.then_inc(B_lo_ready, 1)
                if ahead.exists:
                    act.wait_ge(T_ready, ahead.count(1))
                    act.activation(hT_hi[:, :, :], ps_T, ACT.Relu).then_inc(hT_hi_ready, 1)
                if done.exists:
                    for c in range(NC):
                        act.wait_ge(qf_ready, done.count(NC, c + 1))
                        act.activation(q_hi[:, c, :], q[:, c, :], ACT.Copy).then_inc(q_hi_ready, 1)
                elif b.exists:
                    w2_hi()
                if b.exists:
                    for c in range(NC):
                        act.wait_ge(conv1_ready, b.count(NC, c + 1))
                        act.activation(g[:, c, :], g[:, c, :], ACT.Relu, accum_out=gsum[:, c:c + 1]).then_inc(g_ready, 1)
                if ahead.exists:
                    act.wait_ge(adj_loaded[ahead.slot], ahead.dma_count())
                    if first.exists:
                        act.wait_ge(R_ready, first.count(NC))
                    act.activation(adj_hi[:, :, :], adjT_s[ahead.slot][:, :, :], ACT.Copy).then_inc(adj_hi_ready, 1)
                if first.exists:
                    if done.exists:
                        act.wait_ge(y_ready, done.count(1))
                    copy_A(0)
                if b.exists:
                    copy_gT(0)
                if first.exists:
                    copy_A(1)
                    if not b.exists:
                        w1_hi_and_w2_scale()
                if b.exists:
                    copy_gT(1)
                    act.wait_ge(g_ready, b.count(NC))
                    act.activation(nmean3[:, :], gsum[:, :], ACT.Copy,
                                   scale=-(HID ** -1.5)).then_inc(nmean3_ready, 1)
                if first.exists:
                    act.wait_ge(norm2_ready, first.count(1))
                    for c in range(NC):
                        i = act.activation(h2[:, c, :], x1[:, c, :], ACT.Relu, scale=rstd2[:, c:c + 1],
                                           bias=nmr2[:, c:c + 1])
                    i.then_inc(h2_ready, 1)
                if ahead.exists:
                    copy_QV(0)
                if first.exists:
                    act.wait_ge(h2_ready, first.count(1))
                    act.activation(h2_hi[:, :, :], h2[:, :, :], ACT.Copy).then_inc(h2_hi_ready, 1)
                if ahead.exists:
                    copy_QV(1)
                if b.exists:
                    act.wait_ge(nmean3_ready, b.count(1))
                    for c in range(NC):
                        i = act.activation(squares[:, c, :], g[:, c, :], ACT.Square, scale=HID ** -0.5,
                                           bias=nmean3[:, c:c + 1], accum_out=var3[:, c:c + 1])
                    i.then_inc(var3_ready, 1)
                if ahead.exists:
                    act.wait_ge(Be_ready, ahead.count(1))
                    if first.exists:
                        act.wait_ge(A_ready, first.count(NC))
                    act.activation(B_hi[:, :, N:N + 1], adjT_s[ahead.slot][:, :, 0:1], ACT.Copy)
                    for c in range(NC):
                        i = act.activation(B_hi[:, c, 0:N], HT[:, c, :].bitcast(F32), ACT.Copy, scale=Be[:, c:c + 1])
                    i.then_inc(B_hi_ready, 1)

            run(act, step, {-2: wab})

        @block.vector
        def _(dve):
            def wab():
                dve.wait_ge(wab_hi_ready, 1)
                dve.tensor_tensor(Wab_lo[:, :, :], WabT_raw[:, :, :], Wab_hi[:, :, :].bitcast(F32),
                                  ALU.subtract).then_inc(wab_ready, 1)

            def w2_centre():
                dve.wait_ge(w2_sums_ready, 1)
                for o in range(HC):
                    dve.tensor_tensor(W2c[:, o, :], W2g[:, o, :], ps_mean[:, 0:F], ALU.subtract)
                dve.tensor_copy(cb_bc[:, :], ps_cb[:, 0:F]).then_inc(w2_centred, 1)

            def step(b):
                done, first, ahead, far = b.plus(-1), b.plus(1), b.plus(2), b.plus(3)

                def low_half(ready, count, out_, whole, hi, lo_ready):
                    dve.wait_ge(ready, count)
                    dve.tensor_tensor(out_, whole, hi.bitcast(F32), ALU.subtract).then_inc(lo_ready, 1)

                def final_q(c):
                    dve.wait_ge(q_ready, done.count(NC, c + 1))
                    dve.scalar_tensor_tensor(out=q[:, c, :], in0=ps_q[c][:, 0:F], scalar=rstd3[:, c:c + 1],
                                             in1=cb_bc[:, :], op0=ALU.mult, op1=ALU.add).then_inc(qf_ready, 1)

                def conv1(c):
                    dve.wait_ge(w1out_ready, b.count(NC, c + 1))
                    dve.scalar_tensor_tensor(out=g[:, c, :], in0=ps_w1[c][:, :], scalar=Dn[b.slot][:, c:c + 1],
                                             in1=b1_bc[:, :], op0=ALU.mult, op1=ALU.add).then_inc(conv1_ready, 1)

                def split_A(c):
                    dve.wait_ge(A_hi_ready, first.count(NC, c + 1))
                    dve.tensor_scalar(D[:, c:c + 1], ps_A[c][:, N:N + 1], TINY, None, ALU.max)
                    dve.tensor_tensor(A_lo[first.slot][:, c, :], ps_A[c][:, 0:N],
                                      A_hi[first.slot][:, c, :].bitcast(F32), ALU.subtract).then_inc(A_lo_ready, 1)

                def relu_hT_low():
                    dve.wait_ge(hT_hi_ready, ahead.count(1))
                    dve.scalar_tensor_tensor(out=hT_lo[:, :, :], in0=ps_T, scalar=0.0, in1=hT_hi[:, :, :].bitcast(F32),
                                             op0=ALU.max, op1=ALU.subtract).then_inc(hT_lo_ready, 1)

                if b.exists:
                    low_half(uT_hi_ready, b.count(1), uT_lo[:, :, :], ps_uT, uT_hi[:, :, :], uT_lo_ready)
                if first.exists:
                    for c in range(NC):
                        dve.wait_ge(R_ready, first.count(NC, c + 1))
                        i = dve.tensor_scalar(deg[:, c:c + 1], ps_R[c][:, F:F + 1], EPS_DEG, None, ALU.max)
                    i.then_inc(deg_ready, 1)
                if done.exists:
                    dve.wait_ge(rstd3_ready, done.count(1))
                    final_q(0)
                if first.exists:
                    dve.wait_ge(deg_ready, first.count(1))
                    dve.reciprocal(rdeg[:, :], deg[:, :]).then_inc(rdeg_ready, 1)
                if done.exists:
                    final_q(1)
                if first.exists:
                    dve.wait_ge(rdeg_ready, first.count(1))
                    for c in range(NC):
                        i = dve.scalar_tensor_tensor(out=agg[:, c, :], in0=ps_R[c][:, 0:F], scalar=rdeg[:, c:c + 1],
                                                     in1=Q1[:, c, :], op0=ALU.mult, op1=ALU.add)
                    i.then_inc(agg_ready, 1)
                if ahead.exists and not b.exists:
                    relu_hT_low()
                if b.exists:
                    dve.wait_ge(Dn_ready, b.count(1))
                    conv1(0)
                if first.exists:
                    dve.wait_ge(agg_ready, first.count(1))
                    if b.exists:
                        dve.wait_ge(x1b_ready, b.count(1))
                    dve.scalar_tensor_tensor(out=x1[:, :, :], in0=agg[:, :, :], scalar=0.0,
                                             in1=x_s[first.slot][:, :, :], op0=ALU.max,
                                             op1=ALU.add).then_inc(x1_ready, 1)
                if b.exists:
                    conv1(1)
                if first.exists:
                    dve.wait_ge(x1_ready, first.count(1))
                    for c in range(NC):
                        i = dve.bn_stats(stats2[:, c, :], x1[:, c, :])
                    i.then_inc(stats2_ready, 1)
                    dve.wait_ge(stats2_ready, first.count(1))
                if ahead.exists and b.exists:
                    relu_hT_low()
                if first.exists:
                    for c in range(NC):
                        i = dve.bn_aggr(mv2[:, c, :], stats2[:, c, :])
                    i.then_inc(mv2_ready, 1)
                if ahead.exists:
                    dve.wait_ge(adj_loaded[ahead.slot], ahead.dma_count())
                    if first.exists:
                        dve.wait_ge(A_ready, first.count(NC))
                    for c in range(NC):
                        i = dve.tensor_scalar(HT[:, c, :], adjT_s[ahead.slot][:, c, :], 0.0, None, ALU.not_equal,
                                              ALU.add, accum_out=cnt[:, c:c + 1])
                    i.then_inc(HT_ready, 1)
                if first.exists:
                    split_A(0)
                if ahead.exists:
                    dve.wait_ge(HT_ready, ahead.count(1))
                    dve.tensor_scalar(cnt1[:, :], cnt[:, :], 1.0, None, ALU.max).then_inc(cnt1_ready, 1)
                if b.exists:
                    low_half(gT_hi_ready, b.count(NC, 1), gT_lo[:, 0, :, :], ps_gT[0], gT_hi[:, 0, :, :], gT_lo_ready)
                if first.exists:
                    split_A(1)
                if done.exists:
                    dve.wait_ge(y_ready, done.count(1))
                    dve.wait_ge(ypart_ready, done.count(1))
                    for c in range(NC):
                        i = dve.scalar_tensor_tensor(out=y[done.slot][:, c, :], in0=ps_y[:, c, :],
                                                     scalar=Dn[done.slot][:, c:c + 1], in1=y[done.slot][:, c, :],
                                                     op0=ALU.mult, op1=ALU.add)
                    i.then_inc(y_done, 1)
                if b.exists:
                    low_half(gT_hi_ready, b.count(NC, 2), gT_lo[:, 1, :, :], ps_gT[1], gT_hi[:, 1, :, :], gT_lo_ready)
                if ahead.exists:
                    dve.wait_ge(cnt1_ready, ahead.count(1))
                    dve.reciprocal(Be[:, :], cnt1[:, :]).then_inc(Be_ready, 1)
                if far.exists:
                    dve.wait_ge(x_loaded[far.slot], far.dma_count())
                    for c in range(NC):
                        i = dve.bn_stats(stats1[:, c, :], x_s[far.slot][:, c, :])
                    i.then_inc(stats1_ready, 1)
                    dve.wait_ge(stats1_ready, far.count(1))
                if first.exists:
                    low_half(h2_hi_ready, first.count(1), h2_lo[:, :, :], h2[:, :, :], h2_hi[:, :, :], h2_lo_ready)
                if far.exists:
                    for c in range(NC):
                        i = dve.bn_aggr(mv1[:, c, :], stats1[:, c, :])
                    i.then_inc(mv1_ready, 1)
                if first.exists:
                    dve.wait_ge(A_lo_ready, first.count(NC))
                    dve.reciprocal(Drec[:, :], D[:, :]).then_inc(Drec_ready, 1)
                if ahead.exists:
                    dve.wait_ge(Be_ready, ahead.count(1))
                    dve.tensor_copy(Be_hi[:, :], Be[:, :]).then_inc(Be_hi_ready, 1)
                    low_half(QV_copied, ahead.count(NC, 1), V_lo[:, 0, :], ps_QV[0][:, F:2 * F], V_hi[:, 0, 0:F],
                             V_lo_ready)
                if first.exists:
                    dve.wait_ge(Drec_ready, first.count(1))
                    dve.scalar_tensor_tensor(out=Dn[first.slot][:, :], in0=D[:, :], scalar=TINY, in1=Drec[:, :],
                                             op0=ALU.is_gt, op1=ALU.mult).then_inc(Dn_ready, 1)
                if ahead.exists:
                    low_half(Be_hi_ready, ahead.count(1), Be_lo[:, :], Be[:, :], Be_hi[:, :], Be_lo_ready)
                    low_half(QV_copied, ahead.count(NC, 2), V_lo[:, 1, :], ps_QV[1][:, F:2 * F], V_hi[:, 1, 0:F],
                             V_lo_ready)
                if far.exists:
                    dve.wait_ge(rstd1_ready, far.count(1))
                    if ahead.exists:
                        dve.wait_ge(T_ready, ahead.count(1))
                    for c in range(NC):
                        i = dve.tensor_scalar(z1[:, c, :], x_s[far.slot][:, c, :], nm1[:, c:c + 1],
                                              rstd1[:, c:c + 1], ALU.add, ALU.mult)
                    i.then_inc(z1_ready, 1)

            run(dve, step, {-2: wab, 0: w2_centre})

        @block.tensor
        def _(pe):
            def product(out_, pairs):
                for n, (lhsT, rhs) in enumerate(pairs):
                    i = pe.matmul(out_[:, 0:rhs.shape[-1]], lhsT, rhs, start=n == 0, stop=n == len(pairs) - 1)
                return i

            def three(lhs_hi, lhs_lo, rhs_hi, rhs_lo):
                return [pair for k in range(NC)
                        for pair in ((lhs_hi(k), rhs_hi(k)), (lhs_hi(k), rhs_lo(k)), (lhs_lo(k), rhs_hi(k)))]

            def part(c):
                return slice(c * P, (c + 1) * P)

            def w2_sums():
                pe.wait_ge(w2_scaled, 1)
                product(ps_mean, [(per_hidden[:, :], W2g[:, o, :]) for o in range(HC)])
                product(ps_cb, [(beta_bc[:, o, :], W2T_raw[:, o, :]) for o in range(HC)]).then_inc(w2_sums_ready, 1)

            def start():
                pe.wait_ge(const_ready, 1)
                for _ in range(WARM_UP):
                    pe.transpose(bank[6][:, 0:P], ones[:, :], ident[:, :])

            def step(b):
                done, first, ahead = b.plus(-1), b.plus(1), b.plus(2)

                def A(c):
                    product(ps_A[c], [
                        pair for e in range(NC) for pair in (
                            (HT[:, e, part(c)], B_hi[:, e, :]), (HT[:, e, part(c)], B_lo[:, e, :]))]
                            ).then_inc(A_ready, 1)

                if b.exists:
                    pe.wait_ge(h2_lo_ready, b.count(1))
                    pe.wait_ge(A_lo_ready, b.count(NC))
                    for f in range(NC):
                        i = product(ps_uT[:, f, :], three(
                            lambda k: h2_hi[:, k, part(f)], lambda k: h2_lo[:, k, part(f)],
                            lambda k: A_hi[b.slot][:, k, :], lambda k: A_lo[b.slot][:, k, :]))
                    i.then_inc(uT_ready, 1)
                if first.exists:
                    pe.wait_ge(V_lo_ready, first.count(NC))
                    pe.wait_ge(adj_lo_ready, first.count(1))
                    for c in range(NC):
                        product(ps_R[c], three(
                            lambda k: adj_hi[:, k, part(c)], lambda k: adj_lo[:, k, part(c)],
                            lambda k: V_hi[:, k, :], lambda k: V_lo[:, k, :])).then_inc(R_ready, 1)
                if ahead.exists:
                    pe.wait_ge(z1_ready, ahead.count(1))
                    for f in range(NC):
                        for c in range(NC):
                            i = pe.transpose(ps_T[:, f, part(c)], z1[:, c, part(f)], ident[:, :])
                    i.then_inc(T_ready, 1)
                if first.exists:
                    pe.wait_ge(B_lo_ready, first.count(1))
                    pe.wait_ge(w_lo_ready, first.count(1))
                    A(0)
                if b.exists:
                    pe.wait_ge(uT_lo_ready, b.count(1))
                    if not done.exists:
                        pe.wait_ge(w2_centred, 1)
                        pe.wait_ge(w1_ready, 1)
                    for c in range(NC):
                        if done.exists and c == 1:
                            pe.wait_ge(qf_ready, done.count(NC))
                        product(ps_w1[c], three(
                            lambda f: uT_hi[:, f, part(c)], lambda f: uT_lo[:, f, part(c)],
                            lambda f: W1_hi[:, f, :], lambda f: W1_lo[:, f, :])).then_inc(w1out_ready, 1)
                if first.exists:
                    A(1)
                if done.exists:
                    pe.wait_ge(q_lo_ready, done.count(NC))
                    if b.exists:
                        pe.wait_ge(conv1_ready, b.count(NC, 1))
                    for c in range(NC):
                        i = product(ps_y[:, c, :], three(
                            lambda k: A_hi[done.slot][:, k, part(c)], lambda k: A_lo[done.slot][:, k, part(c)],
                            lambda k: q_hi[:, k, :], lambda k: q_lo[:, k, :]))
                    i.then_inc(y_ready, 1)
                if b.exists:
                    for c in range(NC):
                        pe.wait_ge(g_ready, b.count(NC, c + 1))
                        if first.exists and c == 1:
                            pe.wait_ge(agg_ready, first.count(1))
                        for o in range(HC):
                            i = pe.transpose(ps_gT[c][:, o, :], g[:, c, part(o)], ident[:, :])
                        i.then_inc(gT_ready, 1)
                if ahead.exists:
                    pe.wait_ge(hT_lo_ready, ahead.count(1))
                    if first.exists:
                        pe.wait_ge(agg_ready, first.count(1))
                    else:
                        pe.wait_ge(wab_ready, 1)
                    for c in range(NC):
                        product(ps_QV[c], three(
                            lambda f: hT_hi[:, f, part(c)], lambda f: hT_lo[:, f, part(c)],
                            lambda f: Wab_hi[:, f, :], lambda f: Wab_lo[:, f, :])).then_inc(QV_ready, 1)
                if b.exists:
                    if not done.exists:
                        pe.wait_ge(w2_ready, 1)
                    if first.exists:
                        pe.wait_ge(A_lo_ready, first.count(NC))
                    for c in range(NC):
                        pe.wait_ge(gT_lo_ready, b.count(NC, c + 1))
                        product(ps_q[c], [
                            pair for o in range(HC) for pair in (
                                (gT_hi[:, c, o, :], W2_hi[:, o, :]), (gT_hi[:, c, o, :], W2_lo[:, o, :]),
                                (gT_lo[:, c, o, :], W2_hi[:, o, :]))]).then_inc(q_ready, 1)

            run(pe, step, {-3: start, 0: w2_sums})


def kernel(x, adj, L0_gnn_W, L1_gnn_W1, L1_gnn_b1, L1_gnn_gamma, L1_gnn_beta, L1_gnn_W2, L1_gnn_b2):
    import numpy as np
    import concourse.bacc as bacc
    from concourse.bass_utils import run_bass_kernel_spmd

    x = np.ascontiguousarray(x)
    F = x.shape[2]
    W = np.asarray(L0_gnn_W)
    arrays = {
        "x": x,
        "adjT": np.ascontiguousarray(np.transpose(np.asarray(adj), (0, 2, 1))),
        "WabT": np.ascontiguousarray(W.reshape(W.shape[0], 2, F).transpose(2, 1, 0).reshape(F, -1)),
        "W1T": np.ascontiguousarray(np.asarray(L1_gnn_W1).T),
        "b1": np.ascontiguousarray(L1_gnn_b1),
        "gamma": np.ascontiguousarray(np.asarray(L1_gnn_gamma).reshape(-1, P).T),
        "beta": np.ascontiguousarray(np.asarray(L1_gnn_beta).reshape(-1, P).T),
        "W2T": np.ascontiguousarray(np.asarray(L1_gnn_W2).T),
        "b2": np.ascontiguousarray(L1_gnn_b2),
    }
    nc = bacc.Bacc("TRN2", target_bir_lowering=False, num_devices=1)
    args = [nc.dram_tensor(n, a.shape, mybir.dt.from_np(a.dtype), kind="ExternalInput").ap()
            for n, a in arrays.items()]
    args.append(nc.dram_tensor("out", x.shape, F32, kind="ExternalOutput").ap())
    gnn_two_layers_kernel(nc, *args)
    r = run_bass_kernel_spmd(nc, [arrays], core_ids=[0])
    return r.results[0]["out"]
```
